# Optimizing a Trainium2 kernel written in Bass

```python
import numpy as np
import jax
import jax.numpy as jnp

def _softmax(x, axis=-1):
    return jax.nn.softmax(x, axis=axis)

def _gelu(x):
    return jax.nn.gelu(x, approximate=True)

def _silu(x):
    return jax.nn.silu(x)

def _sigmoid(x):
    return jax.nn.sigmoid(x)

def _layernorm(x, axis=-1, eps=1e-05):
    m = jnp.mean(x, axis=axis, keepdims=True)
    v = jnp.var(x, axis=axis, keepdims=True)
    return (x - m) / jnp.sqrt(v + eps)

def _scatter_add(tgt, idx, src, axis=0):
    return tgt.at[idx].add(src)

def _segment_sum(src, seg, n):
    return jax.ops.segment_sum(src, seg, n)
kernel_name = 'mk_xattn_ffn_d1_seqx_r8_b4d801'

def setup_inputs(seed: int=0):
    np.random.seed(seed)
    _w = jnp.asarray

    def _rec_inputs():
        import jax
        import jax.numpy as jnp
        _rk = jax.random.key(seed)
        x = -0.0002928 + 1 * jax.random.normal(jax.random.fold_in(_rk, 1), (1, 1024, 128), jnp.float32)
        _lenS = 1024 - jax.random.randint(jax.random.fold_in(_rk, 7), (1,), 0, max(1, 1024 // 4) + 1, jnp.int32)
        _lenS2 = 6404 - jax.random.randint(jax.random.fold_in(_rk, 8), (1,), 0, max(1, 6404 // 4) + 1, jnp.int32)
        _ctx_1024P = jax.random.normal(jax.random.fold_in(_rk, 11), (1, 16, 128), jnp.float32)
        _ctx_1024c = jax.random.dirichlet(jax.random.fold_in(_rk, 511), 0.3 * jnp.ones((16,), jnp.float32), (1, 6404))
        _ctx_1024t = jnp.einsum('bsk,bkd->bsd', _ctx_1024c, _ctx_1024P)
        _ctx_1024t = _ctx_1024t * jax.lax.rsqrt(jnp.mean(jnp.square(_ctx_1024t)) + 1e-12) * 0.953939
        ctx_1024 = -1.39393e-06 + 0.999914 * (_ctx_1024t + 0.3 * jax.random.normal(jax.random.fold_in(_rk, 611), (1, 6404, 128), jnp.float32))
        return (x, ctx_1024)
    x, ctx_1024 = _rec_inputs()

    def _L0_xattn_setup():
        import jax, jax.numpy as jnp
        import numpy as np
        import math
        D_MODEL = 128
        NUM_HEADS = 16
        D_K = D_MODEL // NUM_HEADS
        B, SQ, SK = (2, 256, 256)

        def _alibi_bias(seq_len_q: int, seq_len_k: int, dtype) -> jnp.ndarray:
            slopes = jnp.asarray([2.0 ** (-8.0 * (i + 1) / NUM_HEADS) for i in range(NUM_HEADS)], dtype=dtype)
            q_pos = jnp.arange(seq_len_q, dtype=dtype)[:, None]
            k_pos = jnp.arange(seq_len_k, dtype=dtype)[None, :]
            distance = k_pos - q_pos
            return slopes[:, None, None] * distance[None]
        key = jax.random.key(seed)
        ks = jax.random.split(key, 8)
        bound = math.sqrt(6.0 / (D_MODEL + D_MODEL))
        mk = lambda k: jax.random.uniform(k, (D_MODEL, D_MODEL), jnp.float32, -bound, bound)
        return {'query': jax.random.normal(ks[0], (B, SQ, D_MODEL), jnp.float32), 'key': jax.random.normal(ks[1], (B, SK, D_MODEL), jnp.float32), 'value': jax.random.normal(ks[2], (B, SK, D_MODEL), jnp.float32), 'w_q': mk(ks[3]), 'w_k': mk(ks[4]), 'w_v': mk(ks[5]), 'w_o': mk(ks[6]), 'b_o': jnp.zeros((D_MODEL,), jnp.float32)}
    _L0_xattn_all = _L0_xattn_setup()
    _L0_xattn_in = {k: v for k, v in _L0_xattn_all.items() if k in ('w_q', 'w_k', 'w_v', 'w_o', 'b_o')}
    del _L0_xattn_all

    def _L0_ffn_setup():
        import jax, jax.numpy as jnp
        import numpy as np
        D = 128
        H = 512
        E = 64
        K = 3
        B, S = (2, 256)
        C = 64
        key = jax.random.key(seed)
        ks = jax.random.split(key, 6)
        s = 0.02
        return {'x': jax.random.normal(ks[0], (B, S, D), jnp.float32), 'gate_w': jax.random.normal(ks[1], (D, E), jnp.float32) * s, 'gate_b': jnp.zeros((E,), jnp.float32), 'w1': jax.random.normal(ks[2], (E, D, H), jnp.float32) * s, 'b1': jnp.zeros((E, H), jnp.float32), 'w2': jax.random.normal(ks[3], (E, H, D), jnp.float32) * s, 'b2': jnp.zeros((E, D), jnp.float32)}
    _L0_ffn_all = _L0_ffn_setup()
    _L0_ffn_in = {k: v for k, v in _L0_ffn_all.items() if k in ('gate_w', 'gate_b', 'w1', 'b1', 'w2', 'b2')}
    del _L0_ffn_all
    return {'x': x, 'ctx_1024': ctx_1024, 'L0_xattn_w_q': _L0_xattn_in['w_q'], 'L0_xattn_w_k': _L0_xattn_in['w_k'], 'L0_xattn_w_v': _L0_xattn_in['w_v'], 'L0_xattn_w_o': _L0_xattn_in['w_o'], 'L0_xattn_b_o': _L0_xattn_in['b_o'], 'L0_ffn_gate_w': _L0_ffn_in['gate_w'], 'L0_ffn_gate_b': _L0_ffn_in['gate_b'], 'L0_ffn_w1': _L0_ffn_in['w1'], 'L0_ffn_b1': _L0_ffn_in['b1'], 'L0_ffn_w2': _L0_ffn_in['w2'], 'L0_ffn_b2': _L0_ffn_in['b2']}

def reference(x, ctx_1024, L0_xattn_w_q, L0_xattn_w_k, L0_xattn_w_v, L0_xattn_w_o, L0_xattn_b_o, L0_ffn_gate_w, L0_ffn_gate_b, L0_ffn_w1, L0_ffn_b1, L0_ffn_w2, L0_ffn_b2):
    import jax
    import jax.numpy as jnp

    def _L0_xattn_ref(query, key, value, w_q, w_k, w_v, w_o, b_o):
        import jax, jax.numpy as jnp
        import numpy as np
        import math
        D_MODEL = 128
        NUM_HEADS = 16
        D_K = D_MODEL // NUM_HEADS
        B, SQ, SK = (2, 256, 256)

        def _alibi_bias(seq_len_q: int, seq_len_k: int, dtype) -> jnp.ndarray:
            slopes = jnp.asarray([2.0 ** (-8.0 * (i + 1) / NUM_HEADS) for i in range(NUM_HEADS)], dtype=dtype)
            q_pos = jnp.arange(seq_len_q, dtype=dtype)[:, None]
            k_pos = jnp.arange(seq_len_k, dtype=dtype)[None, :]
            distance = k_pos - q_pos
            return slopes[:, None, None] * distance[None]
        b, sq, _ = query.shape
        sk = key.shape[1]
        Q = (query @ w_q.T).reshape(b, sq, NUM_HEADS, D_K).transpose(0, 2, 1, 3)
        K = (key @ w_k.T).reshape(b, sk, NUM_HEADS, D_K).transpose(0, 2, 1, 3)
        V = (value @ w_v.T).reshape(b, sk, NUM_HEADS, D_K).transpose(0, 2, 1, 3)
        scale = math.sqrt(D_K)
        scores = jnp.einsum('bhqd,bhkd->bhqk', Q, K) / scale
        scores = scores + _alibi_bias(sq, sk, scores.dtype)[None]
        attn = jax.nn.softmax(scores, axis=-1)
        ctx = jnp.einsum('bhqk,bhkd->bqhd', attn, V).reshape(b, sq, D_MODEL)
        return ctx @ w_o.T + b_o

    def _L0_ffn_ref(x, gate_w, gate_b, w1, b1, w2, b2):
        import jax, jax.numpy as jnp
        import numpy as np
        D = 128
        H = 512
        E = 64
        K = 3
        B, S = (2, 256)
        C = 64
        xf = x.reshape(-1, D)
        T = xf.shape[0]
        logits = xf @ gate_w + gate_b
        top_l, top_i = jax.lax.top_k(logits, K)
        gates = jax.nn.softmax(top_l, axis=-1)
        fe = top_i.reshape(-1)
        fg = gates.reshape(-1)
        tok = jnp.repeat(jnp.arange(T), K)
        oh = jax.nn.one_hot(fe, E, dtype=jnp.int32)
        pos = (jnp.cumsum(oh, axis=0) * oh).sum(-1) - 1
        valid = pos < C
        buf = jnp.zeros((E, C, D), x.dtype).at[fe, pos].set(xf[tok], mode='drop')
        h = jax.nn.gelu(jnp.einsum('ecd,edh->ech', buf, w1) + b1[:, None, :], approximate=False)
        y = jnp.einsum('ech,ehd->ecd', h, w2) + b2[:, None, :]
        rows = y[fe, jnp.minimum(pos, C - 1)] * (fg * valid.astype(x.dtype))[:, None]
        out = jnp.zeros_like(xf).at[tok].add(rows)
        return out.reshape(x.shape)
    x = x + _L0_xattn_ref(_layernorm(x, axis=-1), ctx_1024, ctx_1024, L0_xattn_w_q, L0_xattn_w_k, L0_xattn_w_v, L0_xattn_w_o, L0_xattn_b_o)
    x = x + _L0_ffn_ref(_layernorm(x, axis=-1), L0_ffn_gate_w, L0_ffn_gate_b, L0_ffn_w1, L0_ffn_b1, L0_ffn_w2, L0_ffn_b2)
    return x

_drawn_inputs = setup_inputs


def setup_inputs(seed=0):
    import zlib

    import numpy as np

    out = dict(_drawn_inputs(seed))
    spreads = {'L0_xattn_b_o': (0.0, 0.1),
     'L0_ffn_gate_b': (0.0, 0.1),
     'L0_ffn_b1': (0.0, 0.8),
     'L0_ffn_b2': (0.0, 0.1)}
    factors = {'L0_ffn_w1': 2.807}
    for name, (base, spread) in spreads.items():
        noise = np.random.default_rng([zlib.crc32(name.encode()), seed]).standard_normal(out[name].shape)
        drawn = base * np.exp(spread * noise) if base else spread * noise
        out[name] = jnp.asarray(drawn.astype(out[name].dtype))
    for name, factor in factors.items():
        out[name] = (out[name] * factor).astype(out[name].dtype)
    return out
```

```python
from contextlib import ExitStack

import numpy as np

import concourse.bass as bass
from concourse import mybir

F32 = mybir.dt.float32
BF16 = mybir.dt.bfloat16
U32 = mybir.dt.uint32
ALU = mybir.AluOpType
ACT = mybir.ActivationFunctionType
AX = mybir.AxisListType
ds = bass.ds

P = 128
D = 128
NH, DK = 16, 8
SQ, SK = 1024, 6404
TILES = SQ // P
KT = 51
SKP = KT * P
HG, QH = 4, 512
NG = (NH // HG) * (SQ // QH)
QT = QH // P
UNITS = HG * QT
ACH = 16
AW = SKP // ACH
IT = KT // 3
VW = DK + 1
ROW_K = DK * 9
ROW_M = ROW_K + 6
ROW_C = 96 - ROW_K
ORDER = "ASSSAVSASSASSAVASSAVSAS"
PER_TURN = 3
assert (ACH - 1) % PER_TURN == 0
PAD = -1e32

E, H, TOPK, CAP = 64, 512, 3, 64
PAIRS = E // 2
HC = H // P
RING = 8
EPS = 1e-5
NCHUNK, CW = 13, 512
LASTW = SKP - (NCHUNK - 1) * CW


def constants():
    bf = mybir.dt.np(BF16)

    def parts(a):
        a = np.asarray(a, np.float32)
        out = []
        for _ in range(3):
            p = a.astype(bf)
            out.append(p)
            a = a - p.astype(np.float32)
        return out

    pos = np.arange(SKP) - (SK - 1)
    low = pos % 32
    high = (pos - low).astype(np.float32)
    low = low.astype(np.float32)
    kc = np.zeros((ROW_C, SKP), np.float32)
    for j in range(3):
        kc[j, :SK] = high[:SK]
        kc[3 + j, :SK] = low[:SK]
        kc[6 + j] = 1.0
    kc[0, SK:] = PAD
    slopes = np.array([2.0 ** (-8.0 * (i + 1) / NH) for i in range(NH)], np.float32)
    qc = np.zeros((ROW_C, NH // HG, SQ // QH, HG, QH), np.float32)
    for j, s in enumerate(parts(slopes)):
        s = s.astype(np.float32).reshape(NH // HG, 1, HG, 1)
        qc[j] = s
        qc[3 + j] = s
    return {
        "c_keys": kc.astype(bf),
        "c_queries": qc.reshape(ROW_C, NG, HG * QH).astype(bf),
        "c_ident": np.eye(P, dtype=np.float32),
        "c_identb": np.eye(P).astype(bf),
        "c_before": np.triu(np.ones((P, P)), 1).astype(bf),
        "c_ones": np.ones((P, P)).astype(bf),
        "c_experts": np.tile(np.arange(E, dtype=np.float32), (P, 1)),
    }


def layer_norm(dve, link, x, y, square, stats, s_var, s_std, n, s_done):
    def view(t):
        return t.rearrange("p (t d) -> p t d", d=D)

    def per_row(i):
        return stats[:, i * TILES:(i + 1) * TILES]

    def spread(i):
        return per_row(i).rearrange("p (t o) -> p t o", o=1).broadcast_to([P, TILES, D])

    link(dve.tensor_reduce(per_row(0), view(x), AX.X, ALU.add))
    link(dve.tensor_scalar(per_row(0), per_row(0), 1.0 / D, None, ALU.mult))
    link(dve.tensor_tensor(view(y), view(x), spread(0), ALU.subtract))
    link(dve.tensor_tensor(square, y, y, ALU.mult))
    dve.tensor_reduce(per_row(1), view(square), AX.X, ALU.add).then_inc(s_var, 1)
    dve.wait_ge(s_std, n)
    link(dve.reciprocal(per_row(3), per_row(2)))
    dve.tensor_tensor(view(y), view(y), spread(3), ALU.mult).then_inc(s_done, 1)


def build(nc, a, out):
    with ExitStack() as ctx:
        def sb(name, shape, dt=F32):
            return ctx.enter_context(nc.sbuf_tensor(name, shape, dt))

        def sem(name):
            return ctx.enter_context(nc.semaphore(name))

        def dram(name, shape, dt=F32):
            return nc.dram_tensor(name, shape, dt, kind="Internal").ap()

        k_parts_d = dram("k_parts_d", (3, P, SKP), BF16)
        q_parts_d = dram("q_parts_d", (3, DK, NG * HG * QH), BF16)
        x_slots_d = dram("x_slots_d", (E * CAP, D))
        y_slots_d = dram("y_slots_d", (E * CAP, D))

        keys = sb("keys", [P, 2 * HG * SKP], BF16)
        queries = sb("queries", [P, NG * HG * QH], BF16)
        values = sb("values", [P, KT * NH * VW])
        probs = sb("probs", [P, 3 * HG * QH])
        vstage = sb("vstage", [P, 3 * HG * 32])
        chunk_max = sb("chunk_max", [P, ACH * UNITS])
        neg_max = sb("neg_max", [P, UNITS])
        max_rest = sb("max_rest", [P, UNITS])
        max_parts = sb("max_parts", [P, P], BF16)
        max_rows = sb("max_rows", [3 * UNITS, P], BF16)
        acc_copy = sb("acc_copy", [P, QH])
        recip = sb("recip", [P, UNITS])
        heads_out = sb("heads_out", [P, NG * QT * HG * DK])
        resid = sb("resid", [P, TILES * D])
        ident = sb("ident", [P, P])
        identb = sb("identb", [P, P], BF16)
        stats = sb("stats", [P, 4 * TILES])
        eps_t = sb("eps_t", [P, 1])
        warm = sb("warm", [P, 1])
        gate_w = sb("gate_w", [D, E])
        gate_b = sb("gate_b", [P, E])
        b1_t = sb("b1_t", [P, E * HC])
        b2_t = sb("b2_t", [E, D])
        experts = sb("experts", [P, E])
        before = sb("before", [P, P], BF16)
        ones = sb("ones", [P, P], BF16)
        wo_t = sb("wo_t", [D, D])
        bo_t = sb("bo_t", [P, D])

        psum = ctx.enter_context(nc.psum_tensor("psum", [P, 8 * 512], F32))

        def bank(n, w=512, o=0):
            return psum[:, n * 512 + o:n * 512 + o + w]

        s_consts = sem("s_consts")
        s_x = sem("s_x")
        s_w = sem("s_w")
        s_ctx = [sem(f"s_ctx{i}") for i in range(2)]
        s_ln = sem("s_ln")
        s_var = sem("s_var")
        s_std = sem("s_std")
        s_xn = sem("s_xn")
        s_xnT_ps = sem("s_xnT_ps")
        s_xnT = sem("s_xnT")
        s_q_ps = sem("s_q_ps")
        s_k_ps = sem("s_k_ps")
        s_v_ps = sem("s_v_ps")
        s_v_done = sem("s_v_done")
        s_p1 = sem("s_p1")
        s_r1 = sem("s_r1")
        s_p2 = sem("s_p2")
        s_p3 = sem("s_p3")
        s_kst = [sem(f"s_kst{i}") for i in range(2)]
        s_qsplit = sem("s_qsplit")
        s_qst = sem("s_qst")
        s_q_loaded = sem("s_q_loaded")
        s_k_loaded = sem("s_k_loaded")
        s_bo = sem("s_bo")
        s_rows = sem("s_rows")
        s_rows2 = sem("s_rows2")
        s_small = sem("s_small")
        s_zeros = sem("s_zeros")
        s_cleared = sem("s_cleared")
        s_w1 = [sem(f"s_w1_{i}") for i in range(RING)]
        s_w2 = [sem(f"s_w2_{i}") for i in range(RING)]
        s_vones = sem("s_vones")
        s_warm = sem("s_warm")
        s_a_scores = sem("s_a_scores")
        s_a_free = sem("s_a_free")
        s_b_scores = sem("s_b_scores")
        s_exp = sem("s_exp")
        s_pv = sem("s_pv")
        s_vst = sem("s_vst")
        s_acc_sb = sem("s_acc_sb")
        s_acc_T = sem("s_acc_T")
        s_recip = sem("s_recip")
        s_acc_free = sem("s_acc_free")
        s_mchain = sem("s_mchain")
        s_m_T = sem("s_m_T")
        s_m_rows = sem("s_m_rows")
        s_m_loaded = sem("s_m_loaded")

        MSTEPS = 5

        place = keys[:].bitcast(F32)
        W1C = 2 * H
        second = HG * SKP // 2
        w1_at = [i * W1C for i in range(RING)]
        w2_at = [(RING + i) * W1C if i < RING // 2 else second + (i - RING // 2) * W1C for i in range(RING)]
        assert (RING + RING // 2) * W1C <= second
        w1 = [place[:, o:o + W1C].rearrange("p (e h) -> p e h", e=2) for o in w1_at]
        w2 = [place[:, o:o + W1C].rearrange("p (e c d) -> p e c d", e=2, d=D) for o in w2_at]

        def load_w1(eng, p, slot):
            eng.dma_start(w1[slot], a["w1"][ds(2 * p, 2)].rearrange("e d h -> d e h")).then_inc(s_w1[slot], 16)

        def load_w2(eng, p, slot):
            eng.dma_start(w2[slot].rearrange("p e c d -> p e (c d)"),
                          a["w2"][ds(2 * p, 2)].rearrange("e (p c) d -> p e (c d)", c=HC)).then_inc(s_w2[slot], 16)

        pctx = ExitStack()
        with pctx:
            late = keys[:, HG * SKP:2 * HG * SKP]
            late32 = late.bitcast(F32)
            ctx_t = late32[:, 0:2 * CW]
            wk_t = late32[:, 1024:1024 + D]
            wv_t = late32[:, 1152:1152 + D]
            wq_t = late32[:, 1280:1280 + D]
            k_split = late[:, 4096:4096 + 2 * 3 * CW]
            q_split = late[:, 8192:8192 + 3 * SQ]
            k_rest = probs[:, 0:2 * CW]
            q_full = probs[:, 2 * CW:2 * CW + SQ]
            xn = probs[:, 2 * CW + SQ:2 * CW + 2 * SQ]
            xnT = probs[:, 2 * CW + 2 * SQ:2 * CW + 3 * SQ]
            x_sq = probs[:, 2 * CW + 3 * SQ:2 * CW + 4 * SQ]

            block = pctx.enter_context(nc.Block())

            def width(c):
                return CW if c < NCHUNK - 1 else LASTW

            @block.sync
            def _(sp):
                sp.dma_start(resid[:].rearrange("p (t d) -> p t d", d=D),
                             a["x"].rearrange("o (t p) d -> p (o t) d", p=P)).then_inc(s_x, 16)
                sp.dma_start(wk_t, a["wk_t"]).then_inc(s_w, 16)
                sp.dma_start(wv_t, a["wv_t"]).then_inc(s_w, 16)
                for c in range(2):
                    sp.dma_start(ctx_t[:, c * CW:(c + 1) * CW],
                                 a["ctx_t"][:, c * CW:(c + 1) * CW]).then_inc(s_ctx[c], 16)
                sp.dma_start(ident[:], a["c_ident"]).then_inc(s_consts, 16)
                sp.dma_start(identb[:], a["c_identb"]).then_inc(s_consts, 16)
                sp.dma_start(wq_t, a["wq_t"]).then_inc(s_consts, 16)
                for c in range(NCHUNK):
                    w, i = width(c), c % 2
                    sp.wait_ge(s_p3, c + 1)
                    sp.dma_start(k_parts_d[:, :, c * CW:c * CW + w].rearrange("j p k -> p j k"),
                                 k_split[:, i * 3 * CW:(i + 1) * 3 * CW]
                                 .rearrange("p (j k) -> p j k", j=3)[:, :, 0:w]).then_inc(s_kst[i], 16)
                    if c + 2 < NCHUNK:
                        w2 = width(c + 2)
                        sp.wait_ge(s_v_ps, c + 1)
                        sp.dma_start(ctx_t[:, i * CW:i * CW + w2],
                                     a["ctx_t"][:, (c + 2) * CW:(c + 2) * CW + w2]).then_inc(s_ctx[i], 16)
                sp.wait_ge(s_qsplit, 4)
                for t in range(NG):
                    g, s = t // 2, t % 2
                    for j in range(3):
                        sp.dma_start(q_parts_d[j, :, t * HG * QH:(t + 1) * HG * QH].rearrange("d (h q) -> h d q", h=HG),
                                     q_split[g * HG * DK:(g + 1) * HG * DK, j * SQ + s * QH:j * SQ + (s + 1) * QH]
                                     ).then_inc(s_qst, 16)
                sp.wait_ge(s_kst[0], 16 * 7)
                sp.wait_ge(s_kst[1], 16 * 6)

                def load_keys(hg):
                    for i in range(3):
                        for j in range(3):
                            r = (i * 3 + j) * DK
                            b = (hg % 2) * HG * SKP
                            sp.dma_start(
                                keys[r:r + DK, b:b + HG * SKP].rearrange("d (h k) -> d h k", h=HG),
                                k_parts_d[j, hg * HG * DK:(hg + 1) * HG * DK, :]
                                .rearrange("(h d) k -> d h k", d=DK)).then_inc(s_k_loaded, 16)

                load_keys(0)
                sp.wait_ge(s_qst, 16 * 3 * NG)
                for i in range(3):
                    for j in range(3):
                        r = (i * 3 + j) * DK
                        sp.dma_start(queries[r:r + DK, :], q_parts_d[i]).then_inc(s_q_loaded, 16)
                sp.wait_ge(s_k_loaded, 16 * 9)
                load_keys(1)

                def max_rows_of(t):
                    sp.wait_ge(s_m_rows, t + 1)
                    for i in range(3):
                        sp.dma_start(queries[ROW_M + i:ROW_M + i + 1, t * HG * QH:(t + 1) * HG * QH]
                                     .rearrange("o (u q) -> o u q", q=P),
                                     max_rows[i * UNITS:(i + 1) * UNITS, :]).then_inc(s_m_loaded, 16)

                for t in range(NG):
                    max_rows_of(t)
                    hg = t // 2 + 1
                    if t % 2 == 0 and t >= 2 and hg < NH // HG:
                        sp.wait_ge(s_pv, 2 * (hg - 1) * KT + 3)
                        load_keys(hg)
                    if t == NG - 2:
                        sp.wait_ge(s_pv, (NG - 2) * KT + 3)
                        for p in range(RING):
                            load_w1(sp, p, p)
                        for p in range(RING // 2):
                            load_w2(sp, p, p)

            @block.gpsimd
            def _(pool):
                pool.dma_start(bo_t[:], a["b_o"].rearrange("(o d) -> o d", o=1).broadcast_to([P, D])).then_inc(s_bo, 16)
                pool.dma_start(queries[ROW_K:96, :], a["c_queries"].rearrange("r g q -> r (g q)")).then_inc(s_rows, 16)
                for b in range(HG):
                    pool.dma_start(keys[ROW_K:96, b * SKP:(b + 1) * SKP], a["c_keys"]).then_inc(s_rows, 16)
                pool.memset(heads_out[:], 0.0).then_inc(s_zeros, 1)
                pool.wait_ge(s_zeros, 1)
                pool.dma_start(x_slots_d.rearrange("(n p) d -> p n d", p=P),
                               heads_out[:, 0:D].rearrange("p (o d) -> p o d", o=1)
                               .broadcast_to([P, E * CAP // P, D])).then_inc(s_cleared, 16)
                vals = values[:].rearrange("p (k h v) -> p k h v", h=NH, v=VW)
                pool.memset(vals[:, :, :, DK], 1.0).then_inc(s_vones, 1)
                pool.wait_ge(s_vones, 1)
                pool.memset(vstage[:], 0.0).then_inc(s_vones, 1)
                pool.wait_ge(s_vones, 2)
                pool.memset(queries[96:P, :].bitcast(F32), 0.0).then_inc(s_vones, 1)
                pool.wait_ge(s_vones, 3)
                pool.memset(keys[96:P, 0:HG * SKP].bitcast(F32), 0.0).then_inc(s_vones, 1)
                for t, n in ((wo_t, "wo_t"), (gate_w, "gate_w"), (b1_t, "b1_t"), (b2_t, "b2"),
                             (experts, "c_experts"), (before, "c_before"), (ones, "c_ones")):
                    pool.dma_start(t[:], a[n]).then_inc(s_small, 16)
                pool.dma_start(gate_b[:], a["gate_b"].rearrange("(o d) -> o d", o=1).broadcast_to([P, E])).then_inc(s_small, 16)
                pool.wait_ge(s_vones, 4)
                pool.wait_ge(s_qst, 16 * 3 * NG)
                pool.wait_ge(s_kst[0], 16 * 7)
                pool.wait_ge(s_kst[1], 16 * 6)
                for b in range(HG, 2 * HG):
                    pool.dma_start(keys[ROW_K:96, b * SKP:(b + 1) * SKP], a["c_keys"]).then_inc(s_rows2, 16)
                pool.memset(keys[96:P, HG * SKP:2 * HG * SKP].bitcast(F32), 0.0).then_inc(s_vones, 1)
                pool.wait_ge(s_vones, 5)
                pool.wait_ge(s_v_done, NCHUNK)
                with pool.Fori(0, NG) as t:
                    hg = pool.snap(t // 2)
                    with pool.Fori(0, IT) as it:
                        for j in range(3):
                            pool.wait_ge(s_pv, t * KT + it * 3 + j + 1)
                            pool.tensor_copy(
                                vstage[:, j * HG * 32:(j + 1) * HG * 32].rearrange("p (h v) -> p h v", v=32)[:, :, 0:VW],
                                values[:, ds(it * (3 * NH * VW) + hg * (HG * VW) + j * NH * VW, HG * VW)]
                                .rearrange("p (h v) -> p h v", v=VW)).then_inc(s_vst, 1)

            @block.scalar
            def _(act):
                act.wait_ge(s_var, 1)
                act.activation(stats[:, 2 * TILES:3 * TILES], stats[:, TILES:2 * TILES], ACT.Sqrt,
                               bias=eps_t[:, 0:1], scale=1.0 / D).then_inc(s_std, 1)
                vals = values[:].rearrange("p (k h v) -> p k h v", h=NH, v=VW)
                act.wait_ge(s_vones, 1)
                for c in range(NCHUNK):
                    w, i = width(c), c % 2
                    act.wait_ge(s_k_ps, c + 1)
                    if c >= 2:
                        act.wait_ge(s_kst[i], 16 * (c // 2))
                    p = k_split[:, i * 3 * CW:(i + 1) * 3 * CW]
                    act.activation(p[:, 0:w], bank(i, w), ACT.Copy).then_inc(s_p1, 1)
                    act.wait_ge(s_v_ps, c + 1)
                    act.activation(vals[:, c * 4:c * 4 + w // P, :, 0:DK],
                                   bank(2 + i, w).rearrange("p (k h d) -> p k h d", h=NH, d=DK),
                                   ACT.Copy).then_inc(s_v_done, 1)
                    act.wait_ge(s_r1, c + 1)
                    act.activation(p[:, CW:CW + w], k_rest[:, i * CW:i * CW + w], ACT.Copy).then_inc(s_p2, 1)
                act.activation(warm[:], eps_t[:], ACT.Exp).then_inc(s_warm, 1)
                act.wait_ge(s_qsplit, 4)
                act.sem_inc(s_exp, 3)
                with act.Fori(0, NG) as t:
                    with act.Fori(0, IT) as it:
                        for j in range(3):
                            act.wait_ge(s_pv, t * KT + it * 3 + j + 1)
                            for h in range(HG):
                                n = j * HG + h
                                act.wait_ge(s_b_scores, t * (KT * HG) + it * (3 * HG) + n + 1)
                                act.activation(probs[:, n * QH:(n + 1) * QH], bank(4 + n % 3),
                                               ACT.Exp).then_inc(s_exp, 1)
                    act.wait_ge(s_pv, (t + 1) * KT + 3)
                    act.activation(acc_copy[:], bank(7), ACT.Copy).then_inc(s_acc_sb, 1)

            @block.vector
            def _(dve):
                count = [0]

                def link(ins):
                    count[0] += 1
                    ins.then_inc(s_ln, 1)
                    dve.wait_ge(s_ln, count[0])

                link(dve.memset(eps_t[:], EPS))
                link(dve.memset(max_parts[:], 0.0))
                dve.wait_ge(s_x, 16)
                layer_norm(dve, link, resid[:], xn, x_sq, stats, s_var, s_std, 1, s_xn)
                dve.wait_ge(s_bo, 16)
                link(dve.tensor_tensor(resid[:].rearrange("p (t d) -> p t d", d=D), resid[:].rearrange("p (t d) -> p t d", d=D),
                                       bo_t[:].rearrange("p (o d) -> p o d", o=1).broadcast_to([P, TILES, D]), ALU.add))
                for c in range(NCHUNK):
                    w, i = width(c), c % 2
                    p = k_split[:, i * 3 * CW:(i + 1) * 3 * CW]
                    dve.wait_ge(s_p1, c + 1)
                    dve.tensor_tensor(k_rest[:, i * CW:i * CW + w], bank(i, w), p[:, 0:w],
                                      ALU.subtract).then_inc(s_r1, 1)
                    dve.wait_ge(s_p2, c + 1)
                    dve.tensor_tensor(p[:, 2 * CW:2 * CW + w], k_rest[:, i * CW:i * CW + w], p[:, CW:CW + w],
                                      ALU.subtract).then_inc(s_p3, 1)
                dve.wait_ge(s_xnT_ps, 1)
                for i in range(2):
                    dve.tensor_copy(xnT[:, i * 512:(i + 1) * 512], bank(4 + i)).then_inc(s_xnT, 1)
                dve.wait_ge(s_q_ps, 2)
                for i in range(2):
                    link(dve.tensor_scalar(q_full[:, i * 512:(i + 1) * 512], bank(6 + i), float(1.0 / np.sqrt(DK)),
                                           None, ALU.mult))
                dve.tensor_copy(q_split[:, 0:SQ], q_full).then_inc(s_qsplit, 1)
                dve.wait_ge(s_qsplit, 1)
                link(dve.tensor_tensor(q_full, q_full, q_split[:, 0:SQ], ALU.subtract))
                dve.tensor_copy(q_split[:, SQ:2 * SQ], q_full).then_inc(s_qsplit, 1)
                dve.wait_ge(s_qsplit, 2)
                dve.tensor_tensor(q_split[:, 2 * SQ:3 * SQ], q_full, q_split[:, SQ:2 * SQ],
                                  ALU.subtract).then_inc(s_qsplit, 2)

                dve.sem_inc(s_a_free, 2)
                dve.sem_inc(s_acc_free, 1)

                def pass_a(t, it):
                    for p in range(UNITS // 2):
                        dve.wait_ge(s_a_scores, t * (ACH * UNITS // 2) + it * (UNITS // 2) + p + 1)
                        src = psum[:, (p % 2) * 1024:(p % 2) * 1024 + 1024].rearrange("q (b k) -> q b k", b=2)
                        dve.tensor_reduce(chunk_max[:, ds(it * UNITS + 2 * p, 2)], src[:, :, 0:AW],
                                          AX.X, ALU.max).then_inc(s_a_free, 1)

                def max_chain(t):
                    base = t * MSTEPS
                    dve.wait_ge(s_a_free, t * (ACH * UNITS // 2) + ACH * UNITS // 2 + 2)
                    dve.tensor_reduce(neg_max[:], chunk_max[:].rearrange("q (c u) -> q u c", u=UNITS),
                                      AX.X, ALU.max, negate=True).then_inc(s_mchain, 1)
                    dve.wait_ge(s_mchain, base + 1)
                    dve.tensor_copy(max_parts[:, 0:UNITS], neg_max[:]).then_inc(s_mchain, 1)
                    dve.wait_ge(s_mchain, base + 2)
                    dve.tensor_tensor(max_rest[:], neg_max[:], max_parts[:, 0:UNITS], ALU.subtract).then_inc(s_mchain, 1)
                    dve.wait_ge(s_mchain, base + 3)
                    dve.tensor_copy(max_parts[:, UNITS:2 * UNITS], max_rest[:]).then_inc(s_mchain, 1)
                    dve.wait_ge(s_mchain, base + 4)
                    dve.tensor_tensor(max_parts[:, 2 * UNITS:3 * UNITS], max_rest[:], max_parts[:, UNITS:2 * UNITS],
                                      ALU.subtract).then_inc(s_mchain, 1)
                    dve.wait_ge(s_m_T, t + 1)
                    if not isinstance(t, int) or t:
                        dve.wait_ge(s_m_loaded, t * 48)
                    dve.tensor_copy(max_rows[:], bank(0).bitcast(BF16)[0:3 * UNITS, 0:P]).then_inc(s_m_rows, 1)

                def normalise(t, g, s):
                    ps = bank(7).rearrange("q (t h v) -> q t h v", t=QT, v=32)
                    dve.wait_ge(s_acc_T, t + 1)
                    dve.reciprocal(recip[:].rearrange("q (t h) -> q t h", t=QT), ps[:, :, :, DK]).then_inc(s_recip, 1)
                    dve.wait_ge(s_recip, t + 1)
                    dve.tensor_tensor(
                        heads_out[:].rearrange("q (s t g h d) -> q g s t h d", s=SQ // QH, t=QT, g=NH // HG, d=DK)[:, g, s],
                        ps[:, :, :, 0:DK],
                        recip[:].rearrange("q (t h o) -> q t h o", t=QT, o=1).broadcast_to([P, QT, HG, DK]),
                        ALU.mult).then_inc(s_acc_free, 1)

                with dve.Fori(0, ACH) as it:
                    pass_a(0, it)
                max_chain(0)
                with dve.Fori(1, NG) as t:
                    with dve.Fori(0, ACH) as it:
                        pass_a(t, it)
                    max_chain(t)
                    normalise(t - 1, dve.snap((t - 1) // 2), dve.snap((t - 1) % 2))
                normalise(NG - 1, NH // HG - 1, 1)

            @block.tensor
            def _(pe):
                pe.wait_ge(s_w, 32)
                for c in range(NCHUNK):
                    w, i = width(c), c % 2
                    pe.wait_ge(s_ctx[i], 16 * (c // 2 + 1))
                    if c >= 2:
                        pe.wait_ge(s_r1, c - 1)
                    pe.matmul(bank(i, w), wk_t, ctx_t[:, i * CW:i * CW + w], start=True, stop=True).then_inc(s_k_ps, 1)
                    if c >= 2:
                        pe.wait_ge(s_v_done, c - 1)
                    for k in range(w // P):
                        v = pe.matmul(bank(2 + i, P, k * P), ctx_t[:, i * CW + k * P:i * CW + (k + 1) * P], wv_t,
                                      start=True, stop=True)
                    v.then_inc(s_v_ps, 1)
                    if c == 5:
                        pe.wait_ge(s_consts, 48)
                        pe.wait_ge(s_xn, 1)
                        for k in range(TILES):
                            v = pe.transpose(bank(4 + k // 4, P, (k % 4) * P), xn[:, k * P:(k + 1) * P], ident[:])
                        v.then_inc(s_xnT_ps, 1)
                pe.wait_ge(s_xnT, 2)
                for k in range(2):
                    pe.matmul(bank(6 + k), wq_t, xnT[:, k * 512:(k + 1) * 512], start=True, stop=True).then_inc(s_q_ps, 1)
                pe.sem_inc(s_pv, 3)

                def a_pair(t, it, kbuf, p):
                    pe.wait_ge(s_a_free, t * (ACH * UNITS // 2) + it * (UNITS // 2) + p + 1)
                    for k in range(2):
                        u = 2 * p + k
                        m = pe.matmul(bank((p % 2) * 2 + k, AW),
                                      queries[:, ds(t * (HG * QH) + u * P, P)],
                                      keys[:, ds(kbuf * (HG * SKP) + it * AW + (u // QT) * SKP, AW)],
                                      start=True, stop=True)
                    m.then_inc(s_a_scores, 1)

                def b_scores(t, it, kbuf, n):
                    j, h = n // HG, n % HG
                    pe.wait_ge(s_exp, t * (KT * HG) + it * (3 * HG) + n + 1)
                    pe.matmul(bank(4 + n % 3),
                              keys[:, ds(kbuf * (HG * SKP) + it * (3 * P) + h * SKP + j * P, P)],
                              queries[:, ds(t * (HG * QH) + h * QH, QH)],
                              start=True, stop=True).then_inc(s_b_scores, 1)

                def pv(t, it, j, first=False, last=False):
                    pe.wait_ge(s_exp, t * (KT * HG) + it * (3 * HG) + (j + 1) * HG + 3)
                    pe.wait_ge(s_vst, t * KT + it * 3 + j + 1)
                    if first:
                        pe.wait_ge(s_acc_free, t + 1)
                    for h in range(HG):
                        m = pe.matmul(psum[h * 32:(h + 1) * 32, 7 * 512:8 * 512],
                                      vstage[:, (j * HG + h) * 32:(j * HG + h + 1) * 32],
                                      probs[:, (j * HG + h) * QH:(j * HG + h + 1) * QH],
                                      start=first, stop=last)
                    m.then_inc(s_pv, 1)

                def max_transpose(t):
                    pe.wait_ge(s_mchain, t * MSTEPS + 5)
                    pe.transpose(bank(0).bitcast(BF16)[:, 0:P], max_parts[:], identb[:]).then_inc(s_m_T, 1)

                def both(ta, tb, it, kba, kbb, first=False, a=True, chain=False):
                    done = {"S": 0, "A": 0, "V": 0}
                    for step in ORDER:
                        n = done[step]
                        done[step] += 1
                        if step == "S":
                            b_scores(tb, it, kbb, n)
                        elif step == "A":
                            if a:
                                a_pair(ta, it, kba, n)
                        elif n:
                            pv(tb, it, n - 1, first=first and n == 1)
                            if chain and n == 1:
                                max_transpose(ta)
                        elif not first:
                            pv(tb, it - 1, 2)

                def finish(t):
                    pv(t, IT - 1, 2, last=True)

                def acc_transposes(t):
                    pe.wait_ge(s_acc_sb, t + 1)
                    for k in range(QT):
                        m = pe.transpose(bank(7, P, k * P), acc_copy[:, k * P:(k + 1) * P], ident[:])
                    m.then_inc(s_acc_T, 1)

                pe.wait_ge(s_rows, 16 * 5)
                pe.wait_ge(s_vones, 4)
                pe.wait_ge(s_q_loaded, 16 * 9)
                pe.wait_ge(s_k_loaded, 16 * 9)
                with pe.Fori(0, ACH) as it:
                    for p in range(UNITS // 2):
                        a_pair(0, it, 0, p)
                max_transpose(0)
                pe.wait_ge(s_rows2, 16 * 4)
                pe.wait_ge(s_vones, 5)
                with pe.Fori(1, NG) as ta:
                    tb = pe.snap(ta - 1)
                    kba = pe.snap((ta // 2) % 2)
                    kbb = pe.snap((tb // 2) % 2)
                    pe.wait_ge(s_k_loaded, (ta // 2 + 1) * (16 * 9))
                    pe.wait_ge(s_m_loaded, ta * 48)
                    both(ta, tb, 0, kba, kbb, first=True)
                    with pe.Fori(0, (ACH - 1) // PER_TURN) as n:
                        for k in range(PER_TURN):
                            both(ta, tb, n * PER_TURN + (k + 1), kba, kbb)
                    both(ta, tb, ACH, kba, kbb, a=False, chain=True)
                    finish(tb)
                    acc_transposes(tb)
                tb = NG - 1
                pe.wait_ge(s_m_loaded, NG * 48)
                both(0, tb, 0, 0, (tb // 2) % 2, first=True, a=False)
                with pe.Fori(1, IT) as it:
                    both(0, tb, it, 0, (tb // 2) % 2, a=False)
                finish(tb)
                acc_transposes(tb)


        at = [second + (RING // 2) * W1C]

        def carve(n):
            at[0] += n
            assert at[0] <= 2 * second
            return place[:, at[0] - n:at[0]]

        x_in = [carve(D) for _ in range(RING)]
        y_out = [carve(D) for _ in range(RING)]
        xT = [carve(P) for _ in range(2)]
        h_rows = [carve(H) for _ in range(2)]
        h_cols = [carve(H) for _ in range(2)]
        h_gelu = [carve(H) for _ in range(2)]
        y_got = carve(TOPK * TILES * D)

        val = values[:]
        heads_T, xf, sq2, xfT = (val[:, i * 1024:(i + 1) * 1024] for i in range(4))
        logits = val[:, 4096:4608]
        work = val[:, 4608:5120]
        prb = probs[:]
        chosen = [prb[:, k * 512:(k + 1) * 512] for k in range(TOPK)]
        weights = prb[:, 1536:2048]
        weights_T = prb[0:E, 2048:3072]
        qry = queries[:].bitcast(F32)
        top8 = qry[:, 0:64]
        expert_f = qry[:, 64:88]
        gates = qry[:, 88:112]
        place_f = qry[:, 112:136]
        slot_f = qry[:, 136:160]
        over = qry[:, 160:184]
        gsum = qry[:, 184:192]
        none_before = (TILES - 1) * E
        counts_pad = queries[:, 1024:1024 + none_before + TILES * E]
        counts = counts_pad[:, none_before:]
        idx8 = queries[:, 2048:2176].bitcast(U32)
        to_slot = queries[:, 2176:2176 + 48].bitcast(U32)
        from_slot = queries[:, 2304:2304 + 48].bitcast(U32)

        s_hT = sem("s_hT")
        s_hT_sb = sem("s_hT_sb")
        s_proj = sem("s_proj")
        s_c = sem("s_c")
        s_var2 = sem("s_var2")
        s_std2 = sem("s_std2")
        s_xf = sem("s_xf")
        s_xfT = sem("s_xfT")
        s_xfT_sb = sem("s_xfT_sb")
        s_logits = sem("s_logits")
        s_top = sem("s_top")
        s_expg = sem("s_expg")
        s_counts = sem("s_counts")
        s_prefix = sem("s_prefix")
        s_slots = sem("s_slots")
        s_sent = sem("s_sent")
        s_wts = sem("s_wts")
        s_wts_T = sem("s_wts_T")
        s_wts_sb = sem("s_wts_sb")
        s_b2 = sem("s_b2")
        s_b2_added = sem("s_b2_added")
        s_xin = [sem(f"s_xin{i}") for i in range(RING)]
        s_yst = [sem(f"s_yst{i}") for i in range(RING)]
        s_xT_ps = sem("s_xT_ps")
        s_xT = sem("s_xT")
        s_h_ps = sem("s_h_ps")
        s_h = sem("s_h")
        s_hc_ps = sem("s_hc_ps")
        s_hc = sem("s_hc")
        s_gelu = sem("s_gelu")
        s_y_ps = sem("s_y_ps")
        s_y = sem("s_y")
        s_got = sem("s_got")
        s_final = sem("s_final")
        s_out = sem("s_out")
        STEPS = PAIRS + 3

        def pipeline(eng, stages):
            def step(turn, u):
                for lag, stage in stages:
                    p = turn * RING + (u - lag)
                    if not isinstance(p, int) or 0 <= p < PAIRS:
                        stage(p, (u - lag) % RING, turn + (u - lag) // RING)

            for u in range(RING):
                step(0, u)
            with eng.Fori(1, PAIRS // RING) as turn:
                for u in range(RING):
                    step(turn, u)
            for u in range(STEPS - PAIRS):
                step(PAIRS // RING, u)

        def reached(eng, s, n):
            if not isinstance(n, int) or n > 0:
                eng.wait_ge(s, n)

        with nc.Block() as block:

            @block.sync
            def _(sp):
                for p in range(RING // 2, RING):
                    load_w2(sp, p, p)
                sp.wait_ge(s_sent, 16 * TOPK * TILES)

                def load_x(p, slot):
                    sp.dma_start(x_in[slot], x_slots_d[ds(p * P, P), :]).then_inc(s_xin[slot], 16)

                def store_y(p, slot):
                    sp.wait_ge(s_y, p + 1)
                    sp.dma_start(y_slots_d[ds(p * P, P), :], y_out[slot]).then_inc(s_yst[slot], 16)

                for p in range(RING):
                    load_x(p, p)
                with sp.Fori(0, PAIRS // RING - 1) as n:
                    p = n * RING
                    for u in range(RING):
                        store_y(p + u, u)
                        load_x(p + (u + RING), u)
                        load_w1(sp, p + (u + RING), u)
                        load_w2(sp, p + (u + RING), u)
                for u in range(RING):
                    store_y(PAIRS - RING + u, u)
                for k in range(2):
                    sp.wait_ge(s_final, 1)
                    if k == 0:
                        sp.dma_start(out.rearrange("o (t p) d -> p (o t) d", p=P),
                                     resid[:].rearrange("p (t d) -> p t d", d=D)).then_inc(s_out, 16)
                sp.wait_ge(s_out, 16)

            @block.gpsimd
            def _(pool):
                pool.wait_ge(s_cleared, 16)
                pool.wait_ge(s_slots, 1)
                for t in range(TILES):
                    for k in range(TOPK):
                        c = k * TILES + t
                        pool.indirect_dma_start(
                            out=x_slots_d, out_offset=bass.IndirectOffsetOnAxis(ap=to_slot[:, c:c + 1], axis=0),
                            in_=xf[:, t * D:(t + 1) * D], in_offset=None,
                            bounds_check=E * CAP - 1, oob_is_err=False).then_inc(s_sent, 16)
                for i in range(RING):
                    pool.wait_ge(s_yst[i], 16 * (PAIRS // RING))
                for t in range(TILES):
                    for k in range(TOPK):
                        c = k * TILES + t
                        pool.indirect_dma_start(
                            out=y_got[:, c * D:(c + 1) * D], out_offset=None,
                            in_=y_slots_d, in_offset=bass.IndirectOffsetOnAxis(ap=from_slot[:, c:c + 1], axis=0),
                            bounds_check=E * CAP - 1, oob_is_err=False).then_inc(s_got, 16)

            @block.scalar
            def _(act):
                for i in range(2):
                    act.wait_ge(s_hT, i + 1)
                    act.activation(heads_T[:, i * 512:(i + 1) * 512], bank(i), ACT.Copy).then_inc(s_hT_sb, 1)
                act.wait_ge(s_var2, 1)
                act.activation(stats[:, 2 * TILES:3 * TILES], stats[:, TILES:2 * TILES], ACT.Sqrt,
                               bias=eps_t[:, 0:1], scale=1.0 / D).then_inc(s_std2, 1)
                for i in range(2):
                    act.wait_ge(s_xfT, i + 1)
                    act.activation(xfT[:, i * 512:(i + 1) * 512], bank(4 + i), ACT.Copy).then_inc(s_xfT_sb, 1)
                act.wait_ge(s_top, 1)
                act.activation(gates, gates, ACT.Exp).then_inc(s_expg, 1)
                act.activation(warm[:], eps_t[:], ACT.Gelu).then_inc(s_warm, 1)

                def copy_h(p, slot, turn):
                    act.wait_ge(s_h_ps, p + 1)
                    reached(act, s_hc_ps, p - 1)
                    act.activation(h_rows[slot % 2], bank(2 + slot % 2), ACT.Copy).then_inc(s_h, 1)

                def gelu(p, slot, turn):
                    act.wait_ge(s_hc, p + 1)
                    reached(act, s_y_ps, p - 1)
                    act.activation(h_gelu[slot % 2], h_cols[slot % 2], ACT.Gelu).then_inc(s_gelu, 1)

                pipeline(act, [(1, copy_h), (2, gelu)])

            @block.vector
            def _(dve):
                count = [0]

                def link(ins):
                    count[0] += 1
                    ins.then_inc(s_c, 1)
                    dve.wait_ge(s_c, count[0])

                def by_tile(t, n):
                    return t.rearrange("p (t n) -> p t n", n=n)

                def spread(t, n):
                    return t.rearrange("p (t o) -> p t o", o=1).broadcast_to([P, t.shape[1], n])

                dve.wait_ge(s_small, 16 * 8)
                link(dve.memset(counts_pad[:, 0:none_before], 0.0))
                for i in range(2):
                    dve.wait_ge(s_proj, i + 1)
                    r = resid[:, i * 512:(i + 1) * 512]
                    link(dve.tensor_tensor(r, r, bank(2 + i), ALU.add))
                layer_norm(dve, link, resid[:], xf, sq2, stats, s_var2, s_std2, 1, s_xf)
                dve.wait_ge(s_logits, 1)
                link(dve.tensor_tensor(by_tile(logits, E), by_tile(bank(6), E),
                                       gate_b[:].rearrange("p (o e) -> p o e", o=1).broadcast_to([P, TILES, E]), ALU.add))
                for t in range(TILES):
                    link(dve.max(top8[:, t * 8:(t + 1) * 8], logits[:, t * E:(t + 1) * E]))
                for t in range(TILES):
                    link(dve.max_index(idx8[:, t * 8:(t + 1) * 8], top8[:, t * 8:(t + 1) * 8],
                                       logits[:, t * E:(t + 1) * E]))
                best = top8.rearrange("p (t k) -> p k t", k=8)
                by_k = gates.rearrange("p (k t) -> p k t", t=TILES)
                dve.tensor_tensor(by_k, best[:, 0:TOPK, :], best[:, 0:1, :].broadcast_to([P, TOPK, TILES]),
                                  ALU.subtract).then_inc(s_top, 1)
                link(dve.tensor_copy(expert_f.rearrange("p (k t) -> p k t", t=TILES),
                                     idx8.rearrange("p (t k) -> p k t", k=8)[:, 0:TOPK, :]))
                for k in range(TOPK):
                    link(dve.tensor_tensor(by_tile(chosen[k], E),
                                           experts[:].rearrange("p (o e) -> p o e", o=1).broadcast_to([P, TILES, E]),
                                           spread(expert_f[:, k * TILES:(k + 1) * TILES], E), ALU.is_equal))
                link(dve.tensor_tensor(work, chosen[0], chosen[1], ALU.add))
                dve.tensor_tensor(counts, work, chosen[2], ALU.add).then_inc(s_counts, 1)
                dve.wait_ge(s_expg, 1)
                link(dve.tensor_reduce(gsum, gates.rearrange("p (k t) -> p t k", t=TILES), AX.X, ALU.add))
                link(dve.reciprocal(gsum, gsum))
                link(dve.tensor_tensor(by_k, by_k, gsum.rearrange("p (o t) -> p o t", o=1)
                                       .broadcast_to([P, TOPK, TILES]), ALU.mult))
                dve.wait_ge(s_prefix, 1)
                for k in range(TOPK):
                    link(dve.tensor_tensor(work, bank(7), chosen[k], ALU.mult))
                    link(dve.tensor_reduce(place_f[:, k * TILES:(k + 1) * TILES], by_tile(work, E), AX.X, ALU.add))
                link(dve.tensor_scalar(over, place_f, float(CAP), None, ALU.is_ge))
                link(dve.tensor_scalar(slot_f, expert_f, float(CAP), None, ALU.mult))
                link(dve.scalar_tensor_tensor(slot_f, over, float(E * CAP), slot_f, ALU.mult, ALU.add))
                dve.tensor_tensor(to_slot, slot_f, place_f, ALU.add).then_inc(s_slots, 1)
                link(dve.tensor_scalar(place_f, place_f, float(CAP - 1), None, ALU.min))
                link(dve.tensor_scalar(slot_f, expert_f, float(CAP), None, ALU.mult))
                link(dve.tensor_tensor(from_slot, slot_f, place_f, ALU.add))
                link(dve.tensor_scalar(over, over, -1.0, 1.0, ALU.mult, ALU.add))
                link(dve.tensor_tensor(gates, gates, over, ALU.mult))
                for k in range(TOPK):
                    dst = weights if k == 0 else work
                    link(dve.tensor_tensor(by_tile(dst, E), by_tile(chosen[k], E),
                                           spread(gates[:, k * TILES:(k + 1) * TILES], E), ALU.mult))
                    if k:
                        link(dve.tensor_tensor(weights, weights, work, ALU.add))
                dve.sem_inc(s_wts, 1)
                for i in range(2):
                    dve.wait_ge(s_wts_T, i + 1)
                    dve.tensor_copy(weights_T[:, i * 512:(i + 1) * 512], bank(4 + i)[0:E, :]).then_inc(s_wts_sb, 1)
                for i in range(2):
                    dve.wait_ge(s_b2, i + 1)
                    r = resid[:, i * 512:(i + 1) * 512]
                    dve.tensor_tensor(r, r, bank(2 + i), ALU.add).then_inc(s_b2_added, 1)

                def copy_x(p, slot, turn):
                    dve.wait_ge(s_xT_ps, p + 1)
                    reached(dve, s_h_ps, p - 1)
                    dve.tensor_copy(xT[slot % 2], bank(slot % 2, P)).then_inc(s_xT, 1)

                def bias(p, slot, turn):
                    dve.wait_ge(s_hc_ps, p + 1)
                    reached(dve, s_gelu, p - 1)
                    dve.tensor_tensor(
                        h_cols[slot % 2].rearrange("h (c e s) -> h c e s", c=HC, e=2),
                        bank(4 + slot % 2).rearrange("h (c e s) -> h c e s", c=HC, e=2),
                        b1_t[:, ds(p * (2 * HC), 2 * HC)].rearrange("h (e c o) -> h c e o", e=2, o=1)
                        .broadcast_to([P, HC, 2, CAP]), ALU.add).then_inc(s_hc, 1)

                def copy_y(p, slot, turn):
                    dve.wait_ge(s_y_ps, p + 1)
                    reached(dve, s_yst[slot], turn * 16)
                    dve.tensor_copy(y_out[slot], bank(6 + slot % 2, D)).then_inc(s_y, 1)

                pipeline(dve, [(0, copy_x), (2, bias), (3, copy_y)])
                dve.wait_ge(s_b2_added, 2)
                done = 0
                for t in range(TILES):
                    for k in range(TOPK):
                        c = k * TILES + t
                        if k == 0:
                            dve.wait_ge(s_got, 16 * TOPK * TILES)
                        r = resid[:, t * D:(t + 1) * D]
                        ins = dve.scalar_tensor_tensor(r, y_got[:, c * D:(c + 1) * D], gates[:, c:c + 1], r,
                                                       ALU.mult, ALU.add)
                        if t == TILES - 1 and k == TOPK - 1:
                            ins.then_inc(s_final, 1)
                        else:
                            link(ins)

            @block.tensor
            def _(pe):
                for i in range(2):
                    for k in range(4):
                        m = pe.transpose(bank(i, P, k * P), heads_out[:, (i * 4 + k) * D:(i * 4 + k + 1) * D], ident[:])
                    m.then_inc(s_hT, 1)
                pe.wait_ge(s_small, 16 * 8)
                for i in range(2):
                    pe.wait_ge(s_hT_sb, i + 1)
                    for k in range(4):
                        m = pe.matmul(bank(2 + i, D, k * D), heads_T[:, (i * 4 + k) * P:(i * 4 + k + 1) * P], wo_t[:],
                                      start=True, stop=True)
                    m.then_inc(s_proj, 1)
                pe.wait_ge(s_xf, 1)
                for i in range(2):
                    for k in range(4):
                        t = i * 4 + k
                        m = pe.transpose(bank(4 + i, P, k * P), xf[:, t * D:(t + 1) * D], ident[:])
                    m.then_inc(s_xfT, 1)
                pe.wait_ge(s_xfT_sb, 2)
                for t in range(TILES):
                    m = pe.matmul(bank(6, E, t * E), xfT[:, t * P:(t + 1) * P], gate_w[:], start=True, stop=True)
                m.then_inc(s_logits, 1)
                pe.wait_ge(s_counts, 1)
                pe.matmul(bank(7), before[:], counts, start=True, stop=False)
                for s in range(1, TILES):
                    m = pe.matmul(bank(7), ones[:], counts_pad[:, none_before - s * E:none_before + (TILES - s) * E],
                                  start=False, stop=(s == TILES - 1))
                m.then_inc(s_prefix, 1)
                pe.wait_ge(s_wts, 1)
                for i in range(2):
                    for k in range(4):
                        t = i * 4 + k
                        m = pe.transpose(bank(4 + i, P, k * P)[0:E, :], weights[:, t * E:(t + 1) * E], ident[:])
                    m.then_inc(s_wts_T, 1)
                for i in range(2):
                    pe.wait_ge(s_wts_sb, i + 1)
                    for k in range(4):
                        m = pe.matmul(bank(2 + i, D, k * D), weights_T[:, (i * 4 + k) * P:(i * 4 + k + 1) * P], b2_t[:],
                                      start=True, stop=True)
                    m.then_inc(s_b2, 1)
                pe.wait_ge(s_b2_added, 2)

                def x_transpose(p, slot, turn):
                    pe.wait_ge(s_xin[slot], (turn + 1) * 16)
                    reached(pe, s_xT, p - 1)
                    pe.transpose(bank(slot % 2, P), x_in[slot], ident[:]).then_inc(s_xT_ps, 1)

                def layer1(p, slot, turn):
                    pe.wait_ge(s_xT, p + 1)
                    pe.wait_ge(s_w1[slot], (turn + 1) * 16)
                    reached(pe, s_h, p - 1)
                    for e in range(2):
                        m = pe.matmul(bank(2 + slot % 2)[e * CAP:(e + 1) * CAP, :], xT[slot % 2][:, e * CAP:(e + 1) * CAP],
                                      w1[slot][:, e, :], start=True, stop=True)
                    m.then_inc(s_h_ps, 1)

                def h_transpose(p, slot, turn):
                    pe.wait_ge(s_h, p + 1)
                    reached(pe, s_hc, p - 1)
                    rows = h_rows[slot % 2].rearrange("s (h c) -> s c h", c=HC)
                    for c in range(HC):
                        m = pe.transpose(bank(4 + slot % 2, P, c * P), rows[:, c, :], ident[:])
                    m.then_inc(s_hc_ps, 1)

                def layer2(p, slot, turn):
                    pe.wait_ge(s_gelu, p + 1)
                    pe.wait_ge(s_w2[slot], (turn + 1) * 16)
                    reached(pe, s_y, p - 1)
                    for c in range(HC):
                        for e in range(2):
                            m = pe.matmul(bank(6 + slot % 2, D)[e * CAP:(e + 1) * CAP, :],
                                          h_gelu[slot % 2][:, c * P + e * CAP:c * P + (e + 1) * CAP],
                                          w2[slot][:, e, c, :], start=(c == 0), stop=(c == HC - 1))
                    m.then_inc(s_y_ps, 1)

                pipeline(pe, [(0, x_transpose), (1, layer1), (2, h_transpose), (3, layer2)])


_OUTS = [((1, 1024, 128), "float32")]


def kernel(**inputs):
    import numpy as _np
    import concourse.bacc as _bacc
    from concourse import mybir as _mybir
    from concourse.bass_utils import run_bass_kernel_spmd as _run

    nc = _bacc.Bacc("TRN2", target_bir_lowering=False, num_devices=1)
    i = {k: _np.asarray(v) for k, v in inputs.items()}
    ctx_t = _np.zeros((D, SKP), _np.float32)
    ctx_t[:, :SK] = i["ctx_1024"][0].T
    arrays = {
        "x": i["x"],
        "ctx_t": ctx_t,
        "wq_t": i["L0_xattn_w_q"].T,
        "wk_t": i["L0_xattn_w_k"].T,
        "wv_t": i["L0_xattn_w_v"].T,
        "wo_t": i["L0_xattn_w_o"].T,
        "b_o": i["L0_xattn_b_o"],
        "gate_w": i["L0_ffn_gate_w"],
        "gate_b": i["L0_ffn_gate_b"],
        "w1": i["L0_ffn_w1"],
        "b1_t": i["L0_ffn_b1"].reshape(E, P, HC).transpose(1, 0, 2).reshape(P, E * HC),
        "w2": i["L0_ffn_w2"],
        "b2": i["L0_ffn_b2"],
        **constants(),
    }
    arrays = {k: _np.ascontiguousarray(v) for k, v in arrays.items()}
    aps = {k: nc.dram_tensor(f"in_{k}", v.shape, _mybir.dt.from_np(v.dtype), kind="ExternalInput").ap()
           for k, v in arrays.items()}
    shape, dtype = _OUTS[0]
    out = nc.dram_tensor("out", shape, _mybir.dt.from_np(_np.dtype(dtype)), kind="ExternalOutput").ap()
    build(nc, aps, out)
    r = _run(nc, [{f"in_{k}": v for k, v in arrays.items()}], core_ids=[0])
    return r.results[0]["out"]
```

```python
from contextlib import ExitStack

import numpy as np

import concourse.bass as bass
from concourse import mybir

F32 = mybir.dt.float32
BF16 = mybir.dt.bfloat16
U32 = mybir.dt.uint32
ALU = mybir.AluOpType
ACT = mybir.ActivationFunctionType
AX = mybir.AxisListType
ds = bass.ds

P = 128
D = 128
NH, DK = 16, 8
SQ, SK = 1024, 6404
TILES = SQ // P
KT = 51
SKP = KT * P
HG, QH = 4, 512
NG = (NH // HG) * (SQ // QH)
QT = QH // P
UNITS = HG * QT
ACH = 16
AW = SKP // ACH
IT = KT // 3
VW = DK + 1
ROW_K = DK * 9
ROW_M = ROW_K + 6
ROW_C = 96 - ROW_K
ORDER = "ASSSAVSASSASSAVASSAVSAS"
ALONE = "SSSSVSSSSVSSSSV"
PER_TURN = 3
TURN_ALONE = 4
assert (ACH - 1) % PER_TURN == 0 and (IT - 1) % TURN_ALONE == 0 and ACH % TURN_ALONE == 0
PAD = -1e32

E, H, TOPK, CAP = 64, 512, 3, 64
PAIRS = E // 2
HC = H // P
RING = 8
EPS = 1e-5
NCHUNK, CW = 13, 512
LASTW = SKP - (NCHUNK - 1) * CW
KRING = 6
CTX_LOADS = [(0, 1), (1, 4), (4, 8), (8, NCHUNK)]
KEY_PIECES = [((0, 4), (0, 2)), ((4, 8), (2, 5)), ((8, NCHUNK), (5, ACH // 2))]
for _chunks, _turns in KEY_PIECES:
    assert _turns[1] * 2 * AW <= min(_chunks[1] * CW, SKP)
FBUF = 4


def constants():
    bf = mybir.dt.np(BF16)

    def parts(a):
        a = np.asarray(a, np.float32)
        out = []
        for _ in range(3):
            p = a.astype(bf)
            out.append(p)
            a = a - p.astype(np.float32)
        return out

    pos = np.arange(SKP) - (SK - 1)
    low = pos % 32
    high = (pos - low).astype(np.float32)
    low = low.astype(np.float32)
    kc = np.zeros((ROW_C, SKP), np.float32)
    for j in range(3):
        kc[j, :SK] = high[:SK]
        kc[3 + j, :SK] = low[:SK]
        kc[6 + j] = 1.0
    kc[0, SK:] = PAD
    slopes = np.array([2.0 ** (-8.0 * (i + 1) / NH) for i in range(NH)], np.float32)
    qc = np.zeros((ROW_C, SQ // QH, NH, QH), np.float32)
    for j, s in enumerate(parts(slopes)):
        s = s.astype(np.float32).reshape(1, NH, 1)
        qc[j] = s
        qc[3 + j] = s
    return {
        "c_keys": kc.astype(bf),
        "c_queries": qc.reshape(ROW_C, NH * SQ).astype(bf),
        "c_ident": np.eye(P, dtype=np.float32),
        "c_identb": np.eye(P).astype(bf),
        "c_before": np.triu(np.ones((P, P)), 1).astype(bf),
        "c_ones": np.ones((P, P)).astype(bf),
        "c_experts": np.tile(np.arange(E, dtype=np.float32), (P, 1)),
    }


def layer_norm(dve, link, x, y, square, stats, s_var, s_std, n, s_done):
    def view(t):
        return t.rearrange("p (t d) -> p t d", d=D)

    def per_row(i):
        return stats[:, i * TILES:(i + 1) * TILES]

    def spread(i):
        return per_row(i).rearrange("p (t o) -> p t o", o=1).broadcast_to([P, TILES, D])

    link(dve.tensor_reduce(per_row(0), view(x), AX.X, ALU.add))
    link(dve.tensor_scalar(per_row(0), per_row(0), 1.0 / D, None, ALU.mult))
    link(dve.tensor_tensor(view(y), view(x), spread(0), ALU.subtract))
    link(dve.tensor_tensor(square, y, y, ALU.mult))
    dve.tensor_reduce(per_row(1), view(square), AX.X, ALU.add).then_inc(s_var, 1)
    dve.wait_ge(s_std, n)
    link(dve.reciprocal(per_row(3), per_row(2)))
    dve.tensor_tensor(view(y), view(y), spread(3), ALU.mult).then_inc(s_done, 1)


def build(nc, a, out):
    with ExitStack() as ctx:
        def sb(name, shape, dt=F32):
            return ctx.enter_context(nc.sbuf_tensor(name, shape, dt))

        def sem(name):
            return ctx.enter_context(nc.semaphore(name))

        def dram(name, shape, dt=F32):
            return nc.dram_tensor(name, shape, dt, kind="Internal").ap()

        k_parts_d = dram("k_parts_d", (3, P, SKP), BF16)
        q_parts_d = dram("q_parts_d", (3, SQ // QH, P, QH), BF16)
        x_slots_d = dram("x_slots_d", (E * CAP, D))
        y_slots_d = dram("y_slots_d", (E * CAP, D))

        keys = sb("keys", [P, 2 * HG * SKP], BF16)
        queries = sb("queries", [P, NH * SQ], BF16)
        values = sb("values", [P, KT * NH * VW])
        probs = sb("probs", [P, 3 * HG * QH])
        vstage = sb("vstage", [P, 3 * HG * 32])
        chunk_max = sb("chunk_max", [P, ACH * UNITS])
        pair_max = sb("pair_max", [P, UNITS])
        neg_max = sb("neg_max", [P, UNITS])
        max_rest = sb("max_rest", [P, UNITS])
        max_parts = sb("max_parts", [P, P], BF16)
        max_rows = sb("max_rows", [3 * UNITS, P], BF16)
        acc_copy = sb("acc_copy", [P, QH])
        recip = sb("recip", [P, UNITS])
        heads_out = sb("heads_out", [P, NG * QT * HG * DK])
        resid = sb("resid", [P, TILES * D])
        ident = sb("ident", [P, P])
        identb = sb("identb", [P, P], BF16)
        stats = sb("stats", [P, 4 * TILES])
        eps_t = sb("eps_t", [P, 1])
        warm = sb("warm", [P, 1])
        gate_w = sb("gate_w", [D, E])
        gate_b = sb("gate_b", [P, E])
        b1_t = sb("b1_t", [P, E * HC])
        b2_t = sb("b2_t", [E, D])
        experts = sb("experts", [P, E])
        before = sb("before", [P, P], BF16)
        ones = sb("ones", [P, P], BF16)
        wo_t = sb("wo_t", [D, D])
        bo_t = sb("bo_t", [P, D])

        psum = ctx.enter_context(nc.psum_tensor("psum", [P, 8 * 512], F32))

        def bank(n, w=512, o=0):
            return psum[:, n * 512 + o:n * 512 + o + w]

        s_consts = sem("s_consts")
        s_constb = sem("s_constb")
        s_x = sem("s_x")
        s_w = sem("s_w")
        s_ctx = [sem(f"s_ctx{i}") for i in range(len(CTX_LOADS))]
        s_ln = sem("s_ln")
        s_var = sem("s_var")
        s_std = sem("s_std")
        s_xn = sem("s_xn")
        s_xnT_ps = sem("s_xnT_ps")
        s_xnT = sem("s_xnT")
        s_q_ps = sem("s_q_ps")
        s_k_ps = sem("s_k_ps")
        s_v_ps = sem("s_v_ps")
        s_v_done = sem("s_v_done")
        s_p1 = sem("s_p1")
        s_r1 = sem("s_r1")
        s_p2 = sem("s_p2")
        s_p3 = sem("s_p3")
        s_kst = [sem(f"s_kst{i}") for i in range(KRING)]
        s_qsplit = sem("s_qsplit")
        s_qst = sem("s_qst")
        s_q_loaded = [sem(f"s_q_loaded{s}") for s in range(SQ // QH)]
        s_k_piece = [sem(f"s_k_piece{i}") for i in range(len(KEY_PIECES))]
        s_k_loaded = sem("s_k_loaded")
        s_wq = sem("s_wq")
        s_bo = sem("s_bo")
        s_rows = sem("s_rows")
        s_rows2 = sem("s_rows2")
        s_small = sem("s_small")
        s_zeros = sem("s_zeros")
        s_cleared = sem("s_cleared")
        s_w1 = [sem(f"s_w1_{i}") for i in range(RING)]
        s_w2 = [sem(f"s_w2_{i}") for i in range(RING)]
        s_vones = sem("s_vones")
        s_warm = sem("s_warm")
        s_minus_q = sem("s_minus_q")
        s_f_scores = sem("s_f_scores")
        s_f_above = sem("s_f_above")
        s_f_max = sem("s_f_max")
        s_f_seen = sem("s_f_seen")
        s_f_kept = sem("s_f_kept")
        s_a_scores = sem("s_a_scores")
        s_a_free = sem("s_a_free")
        s_b_scores = sem("s_b_scores")
        s_exp = sem("s_exp")
        s_pv = sem("s_pv")
        s_vst = sem("s_vst")
        s_acc_sb = sem("s_acc_sb")
        s_acc_T = sem("s_acc_T")
        s_recip = sem("s_recip")
        s_acc_free = sem("s_acc_free")
        s_mchain = sem("s_mchain")
        s_m_T = sem("s_m_T")
        s_m_rows = sem("s_m_rows")
        s_m_loaded = sem("s_m_loaded")

        MSTEPS = 5

        place = keys[:].bitcast(F32)
        W1C = 2 * H
        second = HG * SKP // 2
        w1_at = [i * W1C for i in range(RING)]
        w2_at = [(RING + i) * W1C if i < RING // 2 else second + (i - RING // 2) * W1C for i in range(RING)]
        assert (RING + RING // 2) * W1C <= second
        w1 = [place[:, o:o + W1C].rearrange("p (e h) -> p e h", e=2) for o in w1_at]
        w2 = [place[:, o:o + W1C].rearrange("p (e c d) -> p e c d", e=2, d=D) for o in w2_at]

        def load_w1(eng, p, slot):
            eng.dma_start(w1[slot], a["w1"][ds(2 * p, 2)].rearrange("e d h -> d e h")).then_inc(s_w1[slot], 16)

        def load_w2(eng, p, slot):
            eng.dma_start(w2[slot].rearrange("p e c d -> p e (c d)"),
                          a["w2"][ds(2 * p, 2)].rearrange("e (p c) d -> p e (c d)", c=HC)).then_inc(s_w2[slot], 16)

        pctx = ExitStack()
        with pctx:
            late = keys[:, HG * SKP:2 * HG * SKP]
            late32 = late.bitcast(F32)
            ctx_t = late32[:, 0:SKP]
            wk_t = late32[:, SKP:SKP + D]
            wv_t = late32[:, SKP + D:SKP + 2 * D]
            wq_t = late32[:, SKP + 2 * D:SKP + 3 * D]
            split_at = 2 * (SKP + 3 * D)
            k_split = [late[:, split_at + i * 3 * CW:split_at + (i + 1) * 3 * CW] for i in range(KRING)]
            q_split = late[:, split_at + KRING * 3 * CW:split_at + KRING * 3 * CW + 3 * SQ]
            k_rest = [probs[:, o:o + CW] for o in (0, CW, 2 * CW + 4 * SQ, 3 * CW + 4 * SQ)]
            q_full = probs[:, 2 * CW:2 * CW + SQ]
            minus_q = probs[:, 2 * CW + SQ:2 * CW + 2 * SQ].bitcast(BF16)[:, 0:HG * QH]
            above = [probs[:, 2 * CW + 2 * SQ + i * CW:2 * CW + 2 * SQ + i * CW + AW] for i in range(FBUF)]
            xn = probs[:, 2 * CW + SQ:2 * CW + 2 * SQ]
            xnT = probs[:, 2 * CW + 2 * SQ:2 * CW + 3 * SQ]
            x_sq = probs[:, 2 * CW + 3 * SQ:2 * CW + 4 * SQ]

            block = pctx.enter_context(nc.Block())

            def width(c):
                return CW if c < NCHUNK - 1 else LASTW

            def first_query(t):
                return (t % 2) * (NH * QH) + (t // 2) * (HG * QH)

            @block.sync
            def _(sp):
                sp.dma_start(resid[:].rearrange("p (t d) -> p t d", d=D),
                             a["x"].rearrange("o (t p) d -> p (o t) d", p=P)).then_inc(s_x, 16)
                sp.dma_start(wk_t, a["wk_t"]).then_inc(s_w, 16)
                sp.dma_start(ident[:], a["c_ident"]).then_inc(s_consts, 16)
                sp.dma_start(wv_t, a["wv_t"]).then_inc(s_w, 16)
                for i, (c0, c1) in enumerate(CTX_LOADS):
                    k0, k1 = c0 * CW, min(c1 * CW, SKP)
                    sp.dma_start(ctx_t[:, k0:k1], a["ctx_t"][:, k0:k1]).then_inc(s_ctx[i], 16)
                    if i == 0:
                        sp.dma_start(wq_t, a["wq_t"]).then_inc(s_wq, 16)
                sp.dma_start(identb[:], a["c_identb"]).then_inc(s_constb, 16)

                def store_k(c):
                    w = width(c)
                    sp.wait_ge(s_p3, c + 1)
                    sp.dma_start(k_parts_d[:, :, c * CW:c * CW + w].rearrange("j p k -> p j k"),
                                 k_split[c % KRING].rearrange("p (j k) -> p j k", j=3)[:, :, 0:w]
                                 ).then_inc(s_kst[c % KRING], 16)

                def load_q():
                    sp.wait_ge(s_qst, 16)
                    for s in range(SQ // QH):
                        for i in range(3):
                            src = q_parts_d[i, s].rearrange("(o d h) q -> o d (h q)", o=1, d=DK)
                            sp.dma_start(queries[i * 3 * DK:(i + 1) * 3 * DK, s * NH * QH:(s + 1) * NH * QH],
                                         src.broadcast_to([3, DK, NH * QH])).then_inc(s_q_loaded[s], 16)

                def load_piece(i):
                    (c0, c1), _ = KEY_PIECES[i]
                    for c in range(max(c0, c1 - KRING), c1):
                        sp.wait_ge(s_kst[c % KRING], 16 * (c // KRING + 1))
                    k0, k1 = c0 * CW, min(c1 * CW, SKP)
                    for r in range(3):
                        sp.dma_start(keys[r * 3 * DK:(r + 1) * 3 * DK, 0:HG * SKP]
                                     .rearrange("r (h k) -> r h k", h=HG)[:, :, k0:k1],
                                     k_parts_d.rearrange("j (d h) k -> (j d) h k", d=DK)[:, 0:HG, k0:k1]
                                     ).then_inc(s_k_piece[i], 16)

                def load_keys(hg):
                    b = (hg % 2) * HG * SKP
                    src = k_parts_d.rearrange("(o j) (d h) k -> o (j d) (h k)", o=1, d=DK)
                    sp.dma_start(keys[0:ROW_K, b:b + HG * SKP],
                                 src[:, :, hg * HG * SKP:(hg + 1) * HG * SKP]
                                 .broadcast_to([3, 3 * DK, HG * SKP])).then_inc(s_k_loaded, 16)

                for c in range(NCHUNK):
                    store_k(c)
                    if c == 1:
                        sp.wait_ge(s_qsplit, 4)
                        sp.dma_start(q_parts_d.rearrange("j s p q -> p (j s) q"),
                                     q_split.rearrange("p (n q) -> p n q", q=QH)).then_inc(s_qst, 16)
                    if c == 3:
                        load_q()
                    for i, ((_, c1), _) in enumerate(KEY_PIECES):
                        if c == min(c1, NCHUNK - 1):
                            load_piece(i)
                load_keys(1)

                def max_rows_of(t):
                    sp.wait_ge(s_m_rows, t + 1)
                    for i in range(3):
                        c = first_query(t)
                        sp.dma_start(queries[ROW_M + i:ROW_M + i + 1, c:c + HG * QH]
                                     .rearrange("o (u q) -> o u q", q=P),
                                     max_rows[i * UNITS:(i + 1) * UNITS, :]).then_inc(s_m_loaded, 16)

                for t in range(NG):
                    max_rows_of(t)
                    hg = t // 2 + 1
                    if t % 2 == 0 and t >= 2 and hg < NH // HG:
                        sp.wait_ge(s_pv, 2 * (hg - 1) * KT + 3)
                        load_keys(hg)
                    if t == NG - 2:
                        sp.wait_ge(s_pv, (NG - 2) * KT + 3)
                        for p in range(RING):
                            load_w1(sp, p, p)
                        for p in range(RING // 2):
                            load_w2(sp, p, p)

            @block.gpsimd
            def _(pool):
                pool.dma_start(bo_t[:], a["b_o"].rearrange("(o d) -> o d", o=1).broadcast_to([P, D])).then_inc(s_bo, 16)
                pool.dma_start(queries[ROW_K:96, :], a["c_queries"]).then_inc(s_rows, 16)
                for b in range(HG):
                    pool.dma_start(keys[ROW_K:96, b * SKP:(b + 1) * SKP], a["c_keys"]).then_inc(s_rows, 16)
                vals = values[:].rearrange("p (k h v) -> p k h v", h=NH, v=VW)
                pool.memset(vals[:, :, :, DK], 1.0).then_inc(s_vones, 1)
                pool.wait_ge(s_vones, 1)
                pool.memset(vstage[:], 0.0).then_inc(s_vones, 1)
                pool.wait_ge(s_vones, 2)
                pool.memset(queries[96:P, :].bitcast(F32), 0.0).then_inc(s_vones, 1)
                pool.wait_ge(s_vones, 3)
                pool.memset(keys[96:P, 0:HG * SKP].bitcast(F32), 0.0).then_inc(s_vones, 1)
                pool.wait_ge(s_vones, 4)
                pool.wait_ge(s_v_done, NCHUNK)
                pool.wait_ge(s_qst, 16)
                for c in range(NCHUNK - KRING, NCHUNK):
                    pool.wait_ge(s_kst[c % KRING], 16 * (c // KRING + 1))
                for b in range(HG, 2 * HG):
                    pool.dma_start(keys[ROW_K:96, b * SKP:(b + 1) * SKP], a["c_keys"]).then_inc(s_rows2, 16)
                pool.memset(keys[96:P, HG * SKP:2 * HG * SKP].bitcast(F32), 0.0).then_inc(s_vones, 1)
                pool.wait_ge(s_vones, 5)
                pool.memset(heads_out[:], 0.0).then_inc(s_zeros, 1)
                pool.wait_ge(s_zeros, 1)
                pool.dma_start(x_slots_d.rearrange("(n p) d -> p n d", p=P),
                               heads_out[:, 0:D].rearrange("p (o d) -> p o d", o=1)
                               .broadcast_to([P, E * CAP // P, D])).then_inc(s_cleared, 16)
                for t, n in ((wo_t, "wo_t"), (gate_w, "gate_w"), (b1_t, "b1_t"), (b2_t, "b2"),
                             (experts, "c_experts"), (before, "c_before"), (ones, "c_ones")):
                    pool.dma_start(t[:], a[n]).then_inc(s_small, 16)
                pool.dma_start(gate_b[:], a["gate_b"].rearrange("(o d) -> o d", o=1).broadcast_to([P, E])).then_inc(s_small, 16)
                with pool.Fori(0, NG) as t:
                    hg = pool.snap(t // 2)
                    with pool.Fori(0, IT) as it:
                        for j in range(3):
                            pool.wait_ge(s_pv, t * KT + it * 3 + j + 1)
                            pool.tensor_copy(
                                vstage[:, j * HG * 32:(j + 1) * HG * 32].rearrange("p (h v) -> p h v", v=32)[:, :, 0:VW],
                                values[:, ds(it * (3 * NH * VW) + hg * (HG * VW) + j * NH * VW, HG * VW)]
                                .rearrange("p (h v) -> p h v", v=VW)).then_inc(s_vst, 1)

            @block.scalar
            def _(act):
                act.wait_ge(s_var, 1)
                act.activation(stats[:, 2 * TILES:3 * TILES], stats[:, TILES:2 * TILES], ACT.Sqrt,
                               bias=eps_t[:, 0:1], scale=1.0 / D).then_inc(s_std, 1)
                vals = values[:].rearrange("p (k h v) -> p k h v", h=NH, v=VW)
                act.wait_ge(s_vones, 1)

                def first_part(c):
                    w, i = width(c), c % 2
                    act.wait_ge(s_k_ps, c + 1)
                    if c >= KRING:
                        act.wait_ge(s_kst[c % KRING], 16 * (c // KRING))
                    act.activation(k_split[c % KRING][:, 0:w], bank(4 + i, w), ACT.Copy).then_inc(s_p1, 1)

                def second_part(c):
                    w = width(c)
                    act.wait_ge(s_r1, c + 1)
                    act.activation(k_split[c % KRING][:, CW:CW + w], k_rest[c % 4][:, 0:w], ACT.Copy).then_inc(s_p2, 1)

                first_part(0)
                for c in range(NCHUNK):
                    w = width(c)
                    act.wait_ge(s_v_ps, c + 1)
                    act.activation(vals[:, c * 4:c * 4 + w // P, :, 0:DK],
                                   bank(6 + c % 2, w).rearrange("p (k h d) -> p k h d", h=NH, d=DK),
                                   ACT.Copy).then_inc(s_v_done, 1)
                    if c + 1 < NCHUNK:
                        first_part(c + 1)
                    second_part(c)
                act.activation(warm[:], eps_t[:], ACT.Exp).then_inc(s_warm, 1)
                act.wait_ge(s_qsplit, 4)
                act.wait_ge(s_rows, 16 * 5)
                act.wait_ge(s_vones, 4)
                act.wait_ge(s_q_loaded[0], 16 * 3)
                act.activation(minus_q, queries[:, 0:HG * QH], ACT.Copy, scale=-1.0).then_inc(s_minus_q, 1)
                with act.Fori(0, ACH // 2) as n:
                    for u in range(UNITS):
                        act.wait_ge(s_f_max, n * UNITS + u + 1)
                        act.wait_ge(s_f_scores, n * UNITS + u + 1)
                        act.activation(above[u % FBUF], bank(2 * (u % FBUF) + 1, AW), ACT.Relu).then_inc(s_f_above, 1)
                act.sem_inc(s_exp, 3)

                def exps(t, it):
                    for j in range(3):
                        act.wait_ge(s_pv, t * KT + it * 3 + j + 1)
                        for h in range(HG):
                            n = j * HG + h
                            act.wait_ge(s_b_scores, t * (KT * HG) + it * (3 * HG) + n + 1)
                            act.activation(probs[:, n * QH:(n + 1) * QH], bank(4 + n % 3),
                                           ACT.Exp).then_inc(s_exp, 1)

                with act.Fori(0, NG) as t:
                    exps(t, 0)
                    with act.Fori(0, (IT - 1) // TURN_ALONE) as n:
                        for k in range(TURN_ALONE):
                            exps(t, n * TURN_ALONE + (k + 1))
                    act.wait_ge(s_pv, (t + 1) * KT + 3)
                    act.activation(acc_copy[:], bank(7), ACT.Copy).then_inc(s_acc_sb, 1)

            @block.vector
            def _(dve):
                count = [0]

                def link(ins):
                    count[0] += 1
                    ins.then_inc(s_ln, 1)
                    dve.wait_ge(s_ln, count[0])

                link(dve.memset(eps_t[:], EPS))
                link(dve.memset(max_parts[:], 0.0))
                link(dve.memset(chunk_max[:, ACH // 2 * UNITS:], -3.0e38))
                dve.wait_ge(s_x, 16)
                layer_norm(dve, link, resid[:], xn, x_sq, stats, s_var, s_std, 1, s_xn)

                def rest_k(c):
                    w, i = width(c), c % 2
                    dve.wait_ge(s_p1, c + 1)
                    dve.tensor_tensor(k_rest[c % 4][:, 0:w], bank(4 + i, w), k_split[c % KRING][:, 0:w],
                                      ALU.subtract).then_inc(s_r1, 1)

                def last_k(c):
                    w, i = width(c), c % 2
                    p = k_split[c % KRING]
                    dve.wait_ge(s_p2, c + 1)
                    dve.tensor_tensor(p[:, 2 * CW:2 * CW + w], k_rest[c % 4][:, 0:w], p[:, CW:CW + w],
                                      ALU.subtract).then_inc(s_p3, 1)

                dve.wait_ge(s_xnT_ps, 1)
                for i in range(2):
                    dve.tensor_copy(xnT[:, i * 512:(i + 1) * 512], bank(i)).then_inc(s_xnT, 1)
                rest_k(0)
                dve.wait_ge(s_q_ps, 2)
                for i in range(2):
                    link(dve.tensor_scalar(q_full[:, i * 512:(i + 1) * 512], bank(2 + i), float(1.0 / np.sqrt(DK)),
                                           None, ALU.mult))
                dve.tensor_copy(q_split[:, 0:SQ], q_full).then_inc(s_qsplit, 1)
                dve.wait_ge(s_qsplit, 1)
                link(dve.tensor_tensor(q_full, q_full, q_split[:, 0:SQ], ALU.subtract))
                dve.tensor_copy(q_split[:, SQ:2 * SQ], q_full).then_inc(s_qsplit, 1)
                dve.wait_ge(s_qsplit, 2)
                dve.tensor_tensor(q_split[:, 2 * SQ:3 * SQ], q_full, q_split[:, SQ:2 * SQ],
                                  ALU.subtract).then_inc(s_qsplit, 2)
                for c in range(NCHUNK):
                    if c + 1 < NCHUNK:
                        rest_k(c + 1)
                    last_k(c)
                dve.wait_ge(s_bo, 16)
                link(dve.tensor_tensor(resid[:].rearrange("p (t d) -> p t d", d=D), resid[:].rearrange("p (t d) -> p t d", d=D),
                                       bo_t[:].rearrange("p (o d) -> p o d", o=1).broadcast_to([P, TILES, D]), ALU.add))

                dve.sem_inc(s_f_max, FBUF)
                dve.sem_inc(s_acc_free, 1)

                def pass_a(t, it):
                    for p in range(UNITS // 2):
                        dve.wait_ge(s_a_scores, (t - 1) * (ACH * UNITS // 2) + it * (UNITS // 2) + p + 1)
                        src = psum[:, (p % 2) * 1024:(p % 2) * 1024 + 1024].rearrange("q (b k) -> q b k", b=2)
                        dve.tensor_reduce(chunk_max[:, ds(it * UNITS + 2 * p, 2)], src[:, :, 0:AW],
                                          AX.X, ALU.max).then_inc(s_a_free, 1)

                def max_chain(t):
                    base = t * MSTEPS
                    if isinstance(t, int):
                        dve.wait_ge(s_f_max, ACH // 2 * UNITS + FBUF)
                    else:
                        dve.wait_ge(s_a_free, t * (ACH * UNITS // 2) + 2)
                    dve.tensor_reduce(neg_max[:], chunk_max[:].rearrange("q (c u) -> q u c", u=UNITS),
                                      AX.X, ALU.max, negate=True).then_inc(s_mchain, 1)
                    dve.wait_ge(s_mchain, base + 1)
                    dve.tensor_copy(max_parts[:, 0:UNITS], neg_max[:]).then_inc(s_mchain, 1)
                    dve.wait_ge(s_mchain, base + 2)
                    dve.tensor_tensor(max_rest[:], neg_max[:], max_parts[:, 0:UNITS], ALU.subtract).then_inc(s_mchain, 1)
                    dve.wait_ge(s_mchain, base + 3)
                    dve.tensor_copy(max_parts[:, UNITS:2 * UNITS], max_rest[:]).then_inc(s_mchain, 1)
                    dve.wait_ge(s_mchain, base + 4)
                    dve.tensor_tensor(max_parts[:, 2 * UNITS:3 * UNITS], max_rest[:], max_parts[:, UNITS:2 * UNITS],
                                      ALU.subtract).then_inc(s_mchain, 1)
                    dve.wait_ge(s_m_T, t + 1)
                    if not isinstance(t, int) or t:
                        dve.wait_ge(s_m_loaded, t * 48)
                    dve.tensor_copy(max_rows[:], bank(0).bitcast(BF16)[0:3 * UNITS, 0:P]).then_inc(s_m_rows, 1)

                def normalise(t, g, s):
                    ps = bank(7).rearrange("q (t h v) -> q t h v", t=QT, v=32)
                    dve.wait_ge(s_acc_T, t + 1)
                    dve.reciprocal(recip[:].rearrange("q (t h) -> q t h", t=QT), ps[:, :, :, DK]).then_inc(s_recip, 1)
                    dve.wait_ge(s_recip, t + 1)
                    dve.tensor_tensor(
                        heads_out[:].rearrange("q (s t g h d) -> q g s t h d", s=SQ // QH, t=QT, g=NH // HG, d=DK)[:, g, s],
                        ps[:, :, :, 0:DK],
                        recip[:].rearrange("q (t h o) -> q t h o", t=QT, o=1).broadcast_to([P, QT, HG, DK]),
                        ALU.mult).then_inc(s_acc_free, 1)

                def pass_a_all(t):
                    with dve.Fori(0, ACH // TURN_ALONE) as n:
                        for k in range(TURN_ALONE):
                            pass_a(t, n * TURN_ALONE + k)

                with dve.Fori(0, ACH // 2) as n:
                    for u in range(UNITS):
                        dve.wait_ge(s_f_above, n * UNITS + u + 1)
                        dve.sem_inc(s_f_seen, 1)
                        dve.tensor_tensor_reduce(out=above[u % FBUF], in0=bank(2 * (u % FBUF), AW), in1=above[u % FBUF],
                                                 scale=1.0, scalar=-3.0e38, op0=ALU.add, op1=ALU.max,
                                                 accum_out=pair_max[:, u:u + 1]).then_inc(s_f_max, 1)
                    dve.wait_ge(s_f_max, n * UNITS + (UNITS + FBUF))
                    dve.tensor_copy(chunk_max[:, ds(n * UNITS, UNITS)], pair_max[:]).then_inc(s_f_kept, 1)
                    dve.wait_ge(s_f_kept, n + 1)
                dve.sem_inc(s_a_free, 2)
                max_chain(0)
                dve.wait_ge(s_cleared, 16)
                with dve.Fori(1, NG) as t:
                    pass_a_all(t)
                    max_chain(t)
                    normalise(t - 1, dve.snap((t - 1) // 2), dve.snap((t - 1) % 2))
                normalise(NG - 1, NH // HG - 1, 1)

            @block.tensor
            def _(pe):
                pe.wait_ge(s_w, 32)

                def project(c):
                    w, i = width(c), c % 2
                    for n, (c0, _) in enumerate(CTX_LOADS):
                        if c == c0:
                            pe.wait_ge(s_ctx[n], 16)
                    if c >= 2:
                        pe.wait_ge(s_r1, c - 1)
                    pe.matmul(bank(4 + i, w), wk_t, ctx_t[:, c * CW:c * CW + w], start=True, stop=True).then_inc(s_k_ps, 1)
                    if c >= 2:
                        pe.wait_ge(s_v_done, c - 1)
                    for k in range(w // P):
                        v = pe.matmul(bank(6 + i, P, k * P), ctx_t[:, c * CW + k * P:c * CW + (k + 1) * P], wv_t,
                                      start=True, stop=True)
                    v.then_inc(s_v_ps, 1)

                project(0)
                project(1)
                pe.wait_ge(s_consts, 16)
                pe.wait_ge(s_xn, 1)
                for k in range(TILES):
                    v = pe.transpose(bank(k // 4, P, (k % 4) * P), xn[:, k * P:(k + 1) * P], ident[:])
                v.then_inc(s_xnT_ps, 1)
                pe.wait_ge(s_wq, 16)
                for k in range(2):
                    pe.wait_ge(s_xnT, k + 1)
                    pe.matmul(bank(2 + k), wq_t, xnT[:, k * 512:(k + 1) * 512], start=True, stop=True).then_inc(s_q_ps, 1)
                for c in range(2, NCHUNK):
                    project(c)
                pe.wait_ge(s_r1, NCHUNK)
                pe.wait_ge(s_v_done, NCHUNK)
                pe.sem_inc(s_pv, 3)
                pe.sem_inc(s_k_loaded, 16)

                def a_pair(t, qa, it, kbuf, p):
                    pe.wait_ge(s_a_free, (t - 1) * (ACH * UNITS // 2) + it * (UNITS // 2) + p + 1)
                    for k in range(2):
                        u = 2 * p + k
                        m = pe.matmul(bank((p % 2) * 2 + k, AW),
                                      queries[:, ds(qa + u * P, P)],
                                      keys[:, ds(kbuf * (HG * SKP) + it * AW + (u // QT) * SKP, AW)],
                                      start=True, stop=True)
                    m.then_inc(s_a_scores, 1)

                def first_pair(n, u):
                    pe.wait_ge(s_f_max, n * UNITS + u + 1)
                    q = queries[:, u * P:(u + 1) * P]
                    ka, kb = (keys[:, ds(n * (2 * AW) + (u // QT) * SKP + k * AW, AW)] for k in range(2))
                    a_bank, diff_bank = (bank(2 * (u % FBUF) + k, AW) for k in range(2))
                    pe.matmul(a_bank, q, ka, start=True, stop=True)
                    pe.matmul(diff_bank, q, kb, start=True, stop=False)
                    pe.matmul(diff_bank, minus_q[:, u * P:(u + 1) * P], ka, start=False, stop=True).then_inc(s_f_scores, 1)

                def b_scores(t, qb, it, kbuf, n):
                    j, h = n // HG, n % HG
                    pe.wait_ge(s_exp, t * (KT * HG) + it * (3 * HG) + n + 1)
                    pe.matmul(bank(4 + n % 3),
                              keys[:, ds(kbuf * (HG * SKP) + it * (3 * P) + h * SKP + j * P, P)],
                              queries[:, ds(qb + h * QH, QH)],
                              start=True, stop=True).then_inc(s_b_scores, 1)

                def pv(t, it, j, first=False, last=False):
                    pe.wait_ge(s_exp, t * (KT * HG) + it * (3 * HG) + (j + 1) * HG + 3)
                    pe.wait_ge(s_vst, t * KT + it * 3 + j + 1)
                    if first:
                        pe.wait_ge(s_acc_free, t + 1)
                    for h in range(HG):
                        m = pe.matmul(psum[h * 32:(h + 1) * 32, 7 * 512:8 * 512],
                                      vstage[:, (j * HG + h) * 32:(j * HG + h + 1) * 32],
                                      probs[:, (j * HG + h) * QH:(j * HG + h + 1) * QH],
                                      start=first, stop=last)
                    m.then_inc(s_pv, 1)

                def max_transpose(t):
                    pe.wait_ge(s_mchain, t * MSTEPS + 5)
                    pe.transpose(bank(0).bitcast(BF16)[:, 0:P], max_parts[:], identb[:]).then_inc(s_m_T, 1)

                def both(ta, tb, it, kba, kbb, qa, qb, first=False, a=True, chain=False):
                    done = {"S": 0, "A": 0, "V": 0}
                    for step in ORDER if a else ALONE:
                        n = done[step]
                        done[step] += 1
                        if step == "S":
                            b_scores(tb, qb, it, kbb, n)
                        elif step == "A":
                            a_pair(ta, qa, it, kba, n)
                        elif n:
                            pv(tb, it, n - 1, first=first and n == 1)
                            if chain and n == 1:
                                max_transpose(ta)
                        elif not first:
                            pv(tb, it - 1, 2)

                def finish(t):
                    pv(t, IT - 1, 2, last=True)

                def acc_transposes(t):
                    pe.wait_ge(s_acc_sb, t + 1)
                    for k in range(QT):
                        m = pe.transpose(bank(7, P, k * P), acc_copy[:, k * P:(k + 1) * P], ident[:])
                    m.then_inc(s_acc_T, 1)

                pe.wait_ge(s_rows, 16 * 5)
                pe.wait_ge(s_vones, 4)
                pe.wait_ge(s_q_loaded[0], 16 * 3)
                pe.wait_ge(s_minus_q, 1)
                for i, (_, (n0, n1)) in enumerate(KEY_PIECES):
                    pe.wait_ge(s_k_piece[i], 16 * 3)
                    with pe.Fori(n0, n1) as n:
                        for u in range(UNITS):
                            first_pair(n, u)
                pe.wait_ge(s_constb, 16)
                max_transpose(0)
                pe.wait_ge(s_q_loaded[1], 16 * 3)
                pe.wait_ge(s_rows2, 16 * 4)
                pe.wait_ge(s_vones, 5)
                with pe.Fori(1, NG) as ta:
                    tb = pe.snap(ta - 1)
                    kba = pe.snap((ta // 2) % 2)
                    kbb = pe.snap((tb // 2) % 2)
                    qa = pe.snap(first_query(ta))
                    qb = pe.snap(first_query(tb))
                    pe.wait_ge(s_k_loaded, (ta // 2 + 1) * 16)
                    pe.wait_ge(s_m_loaded, ta * 48)
                    both(ta, tb, 0, kba, kbb, qa, qb, first=True)
                    with pe.Fori(0, (ACH - 1) // PER_TURN) as n:
                        for k in range(PER_TURN):
                            both(ta, tb, n * PER_TURN + (k + 1), kba, kbb, qa, qb)
                    both(ta, tb, ACH, kba, kbb, qa, qb, a=False, chain=True)
                    finish(tb)
                    acc_transposes(tb)
                tb = NG - 1
                kbb, qb = (tb // 2) % 2, first_query(tb)
                pe.wait_ge(s_m_loaded, NG * 48)
                both(0, tb, 0, 0, kbb, 0, qb, first=True, a=False)
                with pe.Fori(0, (IT - 1) // TURN_ALONE) as n:
                    for k in range(TURN_ALONE):
                        both(0, tb, n * TURN_ALONE + (k + 1), 0, kbb, 0, qb, a=False)
                finish(tb)
                acc_transposes(tb)


        at = [second + (RING // 2) * W1C]

        def carve(n):
            at[0] += n
            assert at[0] <= 2 * second
            return place[:, at[0] - n:at[0]]

        x_in = [carve(D) for _ in range(RING)]
        y_out = [carve(D) for _ in range(RING)]
        xT = [carve(P) for _ in range(2)]
        h_rows = [carve(H) for _ in range(2)]
        h_cols = [carve(H) for _ in range(2)]
        h_gelu = [carve(H) for _ in range(2)]
        y_got = carve(TOPK * TILES * D)

        val = values[:]
        heads_T, xf, sq2, xfT = (val[:, i * 1024:(i + 1) * 1024] for i in range(4))
        logits = val[:, 4096:4608]
        work = val[:, 4608:5120]
        prb = probs[:]
        chosen = [prb[:, k * 512:(k + 1) * 512] for k in range(TOPK)]
        weights = prb[:, 1536:2048]
        weights_T = prb[0:E, 2048:3072]
        qry = queries[:].bitcast(F32)
        top8 = qry[:, 0:64]
        expert_f = qry[:, 64:88]
        gates = qry[:, 88:112]
        place_f = qry[:, 112:136]
        slot_f = qry[:, 136:160]
        over = qry[:, 160:184]
        gsum = qry[:, 184:192]
        none_before = (TILES - 1) * E
        counts_pad = queries[:, 1024:1024 + none_before + TILES * E]
        counts = counts_pad[:, none_before:]
        idx8 = queries[:, 2048:2176].bitcast(U32)
        to_slot = queries[:, 2176:2176 + 48].bitcast(U32)
        from_slot = queries[:, 2304:2304 + 48].bitcast(U32)

        s_hT = sem("s_hT")
        s_hT_sb = sem("s_hT_sb")
        s_proj = sem("s_proj")
        s_c = sem("s_c")
        s_var2 = sem("s_var2")
        s_std2 = sem("s_std2")
        s_xf = sem("s_xf")
        s_xfT = sem("s_xfT")
        s_xfT_sb = sem("s_xfT_sb")
        s_logits = sem("s_logits")
        s_top = sem("s_top")
        s_expg = sem("s_expg")
        s_counts = sem("s_counts")
        s_prefix = sem("s_prefix")
        s_slots = sem("s_slots")
        s_sent = sem("s_sent")
        s_wts = sem("s_wts")
        s_wts_T = sem("s_wts_T")
        s_wts_sb = sem("s_wts_sb")
        s_b2 = sem("s_b2")
        s_b2_added = sem("s_b2_added")
        s_xin = [sem(f"s_xin{i}") for i in range(RING)]
        s_yst = [sem(f"s_yst{i}") for i in range(RING)]
        s_xT_ps = sem("s_xT_ps")
        s_xT = sem("s_xT")
        s_h_ps = sem("s_h_ps")
        s_h = sem("s_h")
        s_hc_ps = sem("s_hc_ps")
        s_hc = sem("s_hc")
        s_gelu = sem("s_gelu")
        s_y_ps = sem("s_y_ps")
        s_y = sem("s_y")
        s_got = sem("s_got")
        s_final = sem("s_final")
        s_out = sem("s_out")
        STEPS = PAIRS + 3

        def pipeline(eng, stages):
            def step(turn, u):
                for lag, stage in stages:
                    p = turn * RING + (u - lag)
                    if not isinstance(p, int) or 0 <= p < PAIRS:
                        stage(p, (u - lag) % RING, turn + (u - lag) // RING)

            for u in range(RING):
                step(0, u)
            with eng.Fori(1, PAIRS // RING) as turn:
                for u in range(RING):
                    step(turn, u)
            for u in range(STEPS - PAIRS):
                step(PAIRS // RING, u)

        def reached(eng, s, n):
            if not isinstance(n, int) or n > 0:
                eng.wait_ge(s, n)

        with nc.Block() as block:

            @block.sync
            def _(sp):
                for p in range(RING // 2, RING):
                    load_w2(sp, p, p)
                sp.wait_ge(s_sent, 16 * TOPK * TILES)

                def load_x(p, slot):
                    sp.dma_start(x_in[slot], x_slots_d[ds(p * P, P), :]).then_inc(s_xin[slot], 16)

                def store_y(p, slot):
                    sp.wait_ge(s_y, p + 1)
                    sp.dma_start(y_slots_d[ds(p * P, P), :], y_out[slot]).then_inc(s_yst[slot], 16)

                for p in range(RING):
                    load_x(p, p)
                with sp.Fori(0, PAIRS // RING - 1) as n:
                    p = n * RING
                    for u in range(RING):
                        store_y(p + u, u)
                        load_x(p + (u + RING), u)
                        load_w1(sp, p + (u + RING), u)
                        load_w2(sp, p + (u + RING), u)
                for u in range(RING):
                    store_y(PAIRS - RING + u, u)
                for k in range(2):
                    sp.wait_ge(s_final, 1)
                    if k == 0:
                        sp.dma_start(out.rearrange("o (t p) d -> p (o t) d", p=P),
                                     resid[:].rearrange("p (t d) -> p t d", d=D)).then_inc(s_out, 16)
                sp.wait_ge(s_out, 16)

            @block.gpsimd
            def _(pool):
                pool.wait_ge(s_cleared, 16)
                pool.wait_ge(s_slots, 1)
                for t in range(TILES):
                    for k in range(TOPK):
                        c = k * TILES + t
                        pool.indirect_dma_start(
                            out=x_slots_d, out_offset=bass.IndirectOffsetOnAxis(ap=to_slot[:, c:c + 1], axis=0),
                            in_=xf[:, t * D:(t + 1) * D], in_offset=None,
                            bounds_check=E * CAP - 1, oob_is_err=False).then_inc(s_sent, 16)
                for i in range(RING):
                    pool.wait_ge(s_yst[i], 16 * (PAIRS // RING))
                for t in range(TILES):
                    for k in range(TOPK):
                        c = k * TILES + t
                        pool.indirect_dma_start(
                            out=y_got[:, c * D:(c + 1) * D], out_offset=None,
                            in_=y_slots_d, in_offset=bass.IndirectOffsetOnAxis(ap=from_slot[:, c:c + 1], axis=0),
                            bounds_check=E * CAP - 1, oob_is_err=False).then_inc(s_got, 16)

            @block.scalar
            def _(act):
                for i in range(2):
                    act.wait_ge(s_hT, i + 1)
                    act.activation(heads_T[:, i * 512:(i + 1) * 512], bank(i), ACT.Copy).then_inc(s_hT_sb, 1)
                act.wait_ge(s_var2, 1)
                act.activation(stats[:, 2 * TILES:3 * TILES], stats[:, TILES:2 * TILES], ACT.Sqrt,
                               bias=eps_t[:, 0:1], scale=1.0 / D).then_inc(s_std2, 1)
                for i in range(2):
                    act.wait_ge(s_xfT, i + 1)
                    act.activation(xfT[:, i * 512:(i + 1) * 512], bank(4 + i), ACT.Copy).then_inc(s_xfT_sb, 1)
                act.wait_ge(s_top, 1)
                act.activation(gates, gates, ACT.Exp).then_inc(s_expg, 1)
                act.activation(warm[:], eps_t[:], ACT.Gelu).then_inc(s_warm, 1)

                def copy_h(p, slot, turn):
                    act.wait_ge(s_h_ps, p + 1)
                    reached(act, s_hc_ps, p - 1)
                    act.activation(h_rows[slot % 2], bank(2 + slot % 2), ACT.Copy).then_inc(s_h, 1)

                def gelu(p, slot, turn):
                    act.wait_ge(s_hc, p + 1)
                    reached(act, s_y_ps, p - 1)
                    act.activation(h_gelu[slot % 2], h_cols[slot % 2], ACT.Gelu).then_inc(s_gelu, 1)

                pipeline(act, [(1, copy_h), (2, gelu)])

            @block.vector
            def _(dve):
                count = [0]

                def link(ins):
                    count[0] += 1
                    ins.then_inc(s_c, 1)
                    dve.wait_ge(s_c, count[0])

                def by_tile(t, n):
                    return t.rearrange("p (t n) -> p t n", n=n)

                def spread(t, n):
                    return t.rearrange("p (t o) -> p t o", o=1).broadcast_to([P, t.shape[1], n])

                dve.wait_ge(s_small, 16 * 8)
                link(dve.memset(counts_pad[:, 0:none_before], 0.0))
                for i in range(2):
                    dve.wait_ge(s_proj, i + 1)
                    r = resid[:, i * 512:(i + 1) * 512]
                    link(dve.tensor_tensor(r, r, bank(2 + i), ALU.add))
                layer_norm(dve, link, resid[:], xf, sq2, stats, s_var2, s_std2, 1, s_xf)
                dve.wait_ge(s_logits, 1)
                link(dve.tensor_tensor(by_tile(logits, E), by_tile(bank(6), E),
                                       gate_b[:].rearrange("p (o e) -> p o e", o=1).broadcast_to([P, TILES, E]), ALU.add))
                for t in range(TILES):
                    link(dve.max(top8[:, t * 8:(t + 1) * 8], logits[:, t * E:(t + 1) * E]))
                for t in range(TILES):
                    link(dve.max_index(idx8[:, t * 8:(t + 1) * 8], top8[:, t * 8:(t + 1) * 8],
                                       logits[:, t * E:(t + 1) * E]))
                best = top8.rearrange("p (t k) -> p k t", k=8)
                by_k = gates.rearrange("p (k t) -> p k t", t=TILES)
                dve.tensor_tensor(by_k, best[:, 0:TOPK, :], best[:, 0:1, :].broadcast_to([P, TOPK, TILES]),
                                  ALU.subtract).then_inc(s_top, 1)
                link(dve.tensor_copy(expert_f.rearrange("p (k t) -> p k t", t=TILES),
                                     idx8.rearrange("p (t k) -> p k t", k=8)[:, 0:TOPK, :]))
                for k in range(TOPK):
                    link(dve.tensor_tensor(by_tile(chosen[k], E),
                                           experts[:].rearrange("p (o e) -> p o e", o=1).broadcast_to([P, TILES, E]),
                                           spread(expert_f[:, k * TILES:(k + 1) * TILES], E), ALU.is_equal))
                link(dve.tensor_tensor(work, chosen[0], chosen[1], ALU.add))
                dve.tensor_tensor(counts, work, chosen[2], ALU.add).then_inc(s_counts, 1)
                dve.wait_ge(s_expg, 1)
                link(dve.tensor_reduce(gsum, gates.rearrange("p (k t) -> p t k", t=TILES), AX.X, ALU.add))
                link(dve.reciprocal(gsum, gsum))
                link(dve.tensor_tensor(by_k, by_k, gsum.rearrange("p (o t) -> p o t", o=1)
                                       .broadcast_to([P, TOPK, TILES]), ALU.mult))
                dve.wait_ge(s_prefix, 1)
                for k in range(TOPK):
                    link(dve.tensor_tensor(work, bank(7), chosen[k], ALU.mult))
                    link(dve.tensor_reduce(place_f[:, k * TILES:(k + 1) * TILES], by_tile(work, E), AX.X, ALU.add))
                link(dve.tensor_scalar(over, place_f, float(CAP), None, ALU.is_ge))
                link(dve.tensor_scalar(slot_f, expert_f, float(CAP), None, ALU.mult))
                link(dve.scalar_tensor_tensor(slot_f, over, float(E * CAP), slot_f, ALU.mult, ALU.add))
                dve.tensor_tensor(to_slot, slot_f, place_f, ALU.add).then_inc(s_slots, 1)
                link(dve.tensor_scalar(place_f, place_f, float(CAP - 1), None, ALU.min))
                link(dve.tensor_scalar(slot_f, expert_f, float(CAP), None, ALU.mult))
                link(dve.tensor_tensor(from_slot, slot_f, place_f, ALU.add))
                link(dve.tensor_scalar(over, over, -1.0, 1.0, ALU.mult, ALU.add))
                link(dve.tensor_tensor(gates, gates, over, ALU.mult))
                for k in range(TOPK):
                    dst = weights if k == 0 else work
                    link(dve.tensor_tensor(by_tile(dst, E), by_tile(chosen[k], E),
                                           spread(gates[:, k * TILES:(k + 1) * TILES], E), ALU.mult))
                    if k:
                        link(dve.tensor_tensor(weights, weights, work, ALU.add))
                dve.sem_inc(s_wts, 1)
                for i in range(2):
                    dve.wait_ge(s_wts_T, i + 1)
                    dve.tensor_copy(weights_T[:, i * 512:(i + 1) * 512], bank(4 + i)[0:E, :]).then_inc(s_wts_sb, 1)
                for i in range(2):
                    dve.wait_ge(s_b2, i + 1)
                    r = resid[:, i * 512:(i + 1) * 512]
                    dve.tensor_tensor(r, r, bank(2 + i), ALU.add).then_inc(s_b2_added, 1)

                def copy_x(p, slot, turn):
                    dve.wait_ge(s_xT_ps, p + 1)
                    reached(dve, s_h_ps, p - 1)
                    dve.tensor_copy(xT[slot % 2], bank(slot % 2, P)).then_inc(s_xT, 1)

                def bias(p, slot, turn):
                    dve.wait_ge(s_hc_ps, p + 1)
                    reached(dve, s_gelu, p - 1)
                    dve.tensor_tensor(
                        h_cols[slot % 2].rearrange("h (c e s) -> h c e s", c=HC, e=2),
                        bank(4 + slot % 2).rearrange("h (c e s) -> h c e s", c=HC, e=2),
                        b1_t[:, ds(p * (2 * HC), 2 * HC)].rearrange("h (e c o) -> h c e o", e=2, o=1)
                        .broadcast_to([P, HC, 2, CAP]), ALU.add).then_inc(s_hc, 1)

                def copy_y(p, slot, turn):
                    dve.wait_ge(s_y_ps, p + 1)
                    reached(dve, s_yst[slot], turn * 16)
                    dve.tensor_copy(y_out[slot], bank(6 + slot % 2, D)).then_inc(s_y, 1)

                pipeline(dve, [(0, copy_x), (2, bias), (3, copy_y)])
                dve.wait_ge(s_b2_added, 2)
                done = 0
                for t in range(TILES):
                    for k in range(TOPK):
                        c = k * TILES + t
                        if k == 0:
                            dve.wait_ge(s_got, 16 * TOPK * TILES)
                        r = resid[:, t * D:(t + 1) * D]
                        ins = dve.scalar_tensor_tensor(r, y_got[:, c * D:(c + 1) * D], gates[:, c:c + 1], r,
                                                       ALU.mult, ALU.add)
                        if t == TILES - 1 and k == TOPK - 1:
                            ins.then_inc(s_final, 1)
                        else:
                            link(ins)

            @block.tensor
            def _(pe):
                for i in range(2):
                    for k in range(4):
                        m = pe.transpose(bank(i, P, k * P), heads_out[:, (i * 4 + k) * D:(i * 4 + k + 1) * D], ident[:])
                    m.then_inc(s_hT, 1)
                pe.wait_ge(s_small, 16 * 8)
                for i in range(2):
                    pe.wait_ge(s_hT_sb, i + 1)
                    for k in range(4):
                        m = pe.matmul(bank(2 + i, D, k * D), heads_T[:, (i * 4 + k) * P:(i * 4 + k + 1) * P], wo_t[:],
                                      start=True, stop=True)
                    m.then_inc(s_proj, 1)
                pe.wait_ge(s_xf, 1)
                for i in range(2):
                    for k in range(4):
                        t = i * 4 + k
                        m = pe.transpose(bank(4 + i, P, k * P), xf[:, t * D:(t + 1) * D], ident[:])
                    m.then_inc(s_xfT, 1)
                pe.wait_ge(s_xfT_sb, 2)
                for t in range(TILES):
                    m = pe.matmul(bank(6, E, t * E), xfT[:, t * P:(t + 1) * P], gate_w[:], start=True, stop=True)
                m.then_inc(s_logits, 1)
                pe.wait_ge(s_counts, 1)
                pe.matmul(bank(7), before[:], counts, start=True, stop=False)
                for s in range(1, TILES):
                    m = pe.matmul(bank(7), ones[:], counts_pad[:, none_before - s * E:none_before + (TILES - s) * E],
                                  start=False, stop=(s == TILES - 1))
                m.then_inc(s_prefix, 1)
                pe.wait_ge(s_wts, 1)
                for i in range(2):
                    for k in range(4):
                        t = i * 4 + k
                        m = pe.transpose(bank(4 + i, P, k * P)[0:E, :], weights[:, t * E:(t + 1) * E], ident[:])
                    m.then_inc(s_wts_T, 1)
                for i in range(2):
                    pe.wait_ge(s_wts_sb, i + 1)
                    for k in range(4):
                        m = pe.matmul(bank(2 + i, D, k * D), weights_T[:, (i * 4 + k) * P:(i * 4 + k + 1) * P], b2_t[:],
                                      start=True, stop=True)
                    m.then_inc(s_b2, 1)
                pe.wait_ge(s_b2_added, 2)

                def x_transpose(p, slot, turn):
                    pe.wait_ge(s_xin[slot], (turn + 1) * 16)
                    reached(pe, s_xT, p - 1)
                    pe.transpose(bank(slot % 2, P), x_in[slot], ident[:]).then_inc(s_xT_ps, 1)

                def layer1(p, slot, turn):
                    pe.wait_ge(s_xT, p + 1)
                    pe.wait_ge(s_w1[slot], (turn + 1) * 16)
                    reached(pe, s_h, p - 1)
                    for e in range(2):
                        m = pe.matmul(bank(2 + slot % 2)[e * CAP:(e + 1) * CAP, :], xT[slot % 2][:, e * CAP:(e + 1) * CAP],
                                      w1[slot][:, e, :], start=True, stop=True)
                    m.then_inc(s_h_ps, 1)

                def h_transpose(p, slot, turn):
                    pe.wait_ge(s_h, p + 1)
                    reached(pe, s_hc, p - 1)
                    rows = h_rows[slot % 2].rearrange("s (h c) -> s c h", c=HC)
                    for c in range(HC):
                        m = pe.transpose(bank(4 + slot % 2, P, c * P), rows[:, c, :], ident[:])
                    m.then_inc(s_hc_ps, 1)

                def layer2(p, slot, turn):
                    pe.wait_ge(s_gelu, p + 1)
                    pe.wait_ge(s_w2[slot], (turn + 1) * 16)
                    reached(pe, s_y, p - 1)
                    for c in range(HC):
                        for e in range(2):
                            m = pe.matmul(bank(6 + slot % 2, D)[e * CAP:(e + 1) * CAP, :],
                                          h_gelu[slot % 2][:, c * P + e * CAP:c * P + (e + 1) * CAP],
                                          w2[slot][:, e, c, :], start=(c == 0), stop=(c == HC - 1))
                    m.then_inc(s_y_ps, 1)

                pipeline(pe, [(0, x_transpose), (1, layer1), (2, h_transpose), (3, layer2)])


_OUTS = [((1, 1024, 128), "float32")]


def kernel(**inputs):
    import numpy as _np
    import concourse.bacc as _bacc
    from concourse import mybir as _mybir
    from concourse.bass_utils import run_bass_kernel_spmd as _run

    nc = _bacc.Bacc("TRN2", target_bir_lowering=False, num_devices=1)
    i = {k: _np.asarray(v) for k, v in inputs.items()}
    ctx_t = _np.zeros((D, SKP), _np.float32)
    ctx_t[:, :SK] = i["ctx_1024"][0].T
    arrays = {
        "x": i["x"],
        "ctx_t": ctx_t,
        "wq_t": i["L0_xattn_w_q"].reshape(NH, DK, D).transpose(2, 1, 0).reshape(D, D),
        "wk_t": i["L0_xattn_w_k"].reshape(NH, DK, D).transpose(2, 1, 0).reshape(D, D),
        "wv_t": i["L0_xattn_w_v"].T,
        "wo_t": i["L0_xattn_w_o"].T,
        "b_o": i["L0_xattn_b_o"],
        "gate_w": i["L0_ffn_gate_w"],
        "gate_b": i["L0_ffn_gate_b"],
        "w1": i["L0_ffn_w1"],
        "b1_t": i["L0_ffn_b1"].reshape(E, P, HC).transpose(1, 0, 2).reshape(P, E * HC),
        "w2": i["L0_ffn_w2"],
        "b2": i["L0_ffn_b2"],
        **constants(),
    }
    arrays = {k: _np.ascontiguousarray(v) for k, v in arrays.items()}
    aps = {k: nc.dram_tensor(f"in_{k}", v.shape, _mybir.dt.from_np(v.dtype), kind="ExternalInput").ap()
           for k, v in arrays.items()}
    shape, dtype = _OUTS[0]
    out = nc.dram_tensor("out", shape, _mybir.dt.from_np(_np.dtype(dtype)), kind="ExternalOutput").ap()
    build(nc, aps, out)
    r = _run(nc, [{f"in_{k}": v for k, v in arrays.items()}], core_ids=[0])
    return r.results[0]["out"]
```

```python
from contextlib import ExitStack

import numpy as np

import concourse.bass as bass
from concourse import mybir

F32 = mybir.dt.float32
BF16 = mybir.dt.bfloat16
U32 = mybir.dt.uint32
ALU = mybir.AluOpType
ACT = mybir.ActivationFunctionType
AX = mybir.AxisListType
ds = bass.ds

P = 128
D = 128
NH, DK = 16, 8
SQ, SK = 1024, 6404
TILES = SQ // P
KT = 51
SKP = KT * P
HG, QH = 4, 512
NG = (NH // HG) * (SQ // QH)
QT = QH // P
UNITS = HG * QT
ACH = 16
AW = SKP // ACH
IT = KT // 3
VW = DK + 1
ROW_K = DK * 9
ROW_M = ROW_K + 6
ROW_C = 96 - ROW_K
ORDER = "ASSSAVSASSASSAVASSAVSAS"
ALONE = "SSSSVSSSSVSSSSV"
HEAD = "ASSSAVSASSATSSAVASSAVSAS"
HEAD_ALONE = "SSSSVSSTSSVSSSSV"
TAIL = "SSSSVSSMSSVSSSSV"
BEFORE_T = HEAD[:HEAD.index("T")].count("A") - 1
PER_TURN = 5
TURN_ALONE = 4
assert (ACH - 1) % PER_TURN == 0 and (IT - 1) % TURN_ALONE == 0 and ACH % TURN_ALONE == 0
PAD = -1e32

E, H, TOPK, CAP = 64, 512, 3, 64
PAIRS = E // 2
HC = H // P
RING = 8
EPS = 1e-5
NCHUNK, CW = 13, 512
LASTW = SKP - (NCHUNK - 1) * CW
KRING = 6
CTX_LOADS = [(0, 1), (1, 4), (4, 8), (8, NCHUNK)]
KEY_PIECES = [((0, 4), (0, 2)), ((4, 8), (2, 5)), ((8, NCHUNK), (5, ACH // 2))]
for _chunks, _turns in KEY_PIECES:
    assert _turns[1] * 2 * AW <= min(_chunks[1] * CW, SKP)
FBUF = 4


def constants():
    bf = mybir.dt.np(BF16)

    def parts(a):
        a = np.asarray(a, np.float32)
        out = []
        for _ in range(3):
            p = a.astype(bf)
            out.append(p)
            a = a - p.astype(np.float32)
        return out

    pos = np.arange(SKP) - (SK - 1)
    low = pos % 32
    high = (pos - low).astype(np.float32)
    low = low.astype(np.float32)
    kc = np.zeros((ROW_C, SKP), np.float32)
    for j in range(3):
        kc[j, :SK] = high[:SK]
        kc[3 + j, :SK] = low[:SK]
        kc[6 + j] = 1.0
    kc[0, SK:] = PAD
    slopes = np.array([2.0 ** (-8.0 * (i + 1) / NH) for i in range(NH)], np.float32)
    qc = np.zeros((ROW_C, SQ // QH, NH, QH), np.float32)
    for j, s in enumerate(parts(slopes)):
        s = s.astype(np.float32).reshape(1, NH, 1)
        qc[j] = s
        qc[3 + j] = s
    return {
        "c_keys": kc.astype(bf),
        "c_queries": qc.reshape(ROW_C, NH * SQ).astype(bf),
        "c_ident": np.eye(P, dtype=np.float32),
        "c_identb": np.eye(P).astype(bf),
        "c_before": np.triu(np.ones((P, P)), 1).astype(bf),
        "c_ones": np.ones((P, P)).astype(bf),
        "c_results": ((np.arange(TILES)[None, None] * TOPK + np.arange(TOPK)[None, :, None]) * P
                      + np.arange(P)[:, None, None]).reshape(P, TOPK * TILES).astype(np.uint32),
        "c_experts": np.tile(np.arange(E, dtype=np.float32), (P, 1)),
    }


def layer_norm(dve, link, x, y, stats, s_var, s_std, n, s_done):
    def tile(z, t):
        return z[:, t * D:(t + 1) * D]

    parts, both, root = stats[:, 0:6 * TILES], stats[:, 6 * TILES:8 * TILES], stats[:, 8 * TILES:9 * TILES]
    for t in range(TILES):
        ins = dve.bn_stats(parts[:, 6 * t:6 * t + 6], tile(x, t))
    link(ins)
    for t in range(TILES):
        ins = dve.bn_aggr(both[:, 2 * t:2 * t + 2], parts[:, 6 * t:6 * t + 6])
    ins.then_inc(s_var, 1)
    dve.wait_ge(s_var, n)
    dve.wait_ge(s_std, n)
    link(dve.reciprocal(root, root))
    for t in range(TILES):
        ins = dve.tensor_scalar(tile(y, t), tile(x, t), both[:, 2 * t:2 * t + 1], root[:, t:t + 1],
                                ALU.subtract, ALU.mult)
    ins.then_inc(s_done, 1)


def build(nc, a, out):
    with ExitStack() as ctx:
        def sb(name, shape, dt=F32):
            return ctx.enter_context(nc.sbuf_tensor(name, shape, dt))

        def sem(name):
            return ctx.enter_context(nc.semaphore(name))

        def dram(name, shape, dt=F32):
            return nc.dram_tensor(name, shape, dt, kind="Internal").ap()

        k_parts_d = dram("k_parts_d", (3, P, SKP), BF16)
        q_parts_d = dram("q_parts_d", (3, SQ // QH, P, QH), BF16)
        x_slots_d = dram("x_slots_d", (E * CAP, D + 1))
        y_tokens_d = dram("y_tokens_d", (SQ * TOPK, D))

        keys = sb("keys", [P, 2 * HG * SKP], BF16)
        queries = sb("queries", [P, NH * SQ], BF16)
        values = sb("values", [P, KT * NH * VW])
        probs = sb("probs", [P, 3 * HG * QH])
        vstage = sb("vstage", [P, 3 * HG * 32])
        chunk_max = sb("chunk_max", [P, ACH * UNITS])
        pair_max = sb("pair_max", [P, UNITS])
        neg_max = sb("neg_max", [P, UNITS])
        max_rest = sb("max_rest", [P, UNITS])
        max_parts = sb("max_parts", [P, P], BF16)
        max_rows = sb("max_rows", [3 * UNITS, P], BF16)
        acc_copy = sb("acc_copy", [P, QH])
        recip = sb("recip", [P, UNITS])
        heads_out = sb("heads_out", [P, NG * QT * HG * DK])
        resid = sb("resid", [P, TILES * D])
        ident = sb("ident", [P, P])
        identb = sb("identb", [P, P], BF16)
        stats = sb("stats", [P, 9 * TILES])
        eps_t = sb("eps_t", [P, 1])
        warm = sb("warm", [P, 1])
        gate_w = sb("gate_w", [D, E])
        gate_b = sb("gate_b", [P, E])
        b1_t = sb("b1_t", [P, E * HC])
        b2_t = sb("b2_t", [E, D])
        experts = sb("experts", [P, E])
        results = sb("results", [P, TOPK * TILES], U32)
        before = sb("before", [P, P], BF16)
        ones = sb("ones", [P, P], BF16)
        wo_t = sb("wo_t", [D, D])
        bo_t = sb("bo_t", [P, D])

        psum = ctx.enter_context(nc.psum_tensor("psum", [P, 8 * 512], F32))

        def bank(n, w=512, o=0):
            return psum[:, n * 512 + o:n * 512 + o + w]

        BANKS = (4, 5, 6)
        LAST_BANKS = (4, 5, 6, 1, 2, 3)

        s_consts = sem("s_consts")
        s_constb = sem("s_constb")
        s_x = sem("s_x")
        s_w = sem("s_w")
        s_ctx = [sem(f"s_ctx{i}") for i in range(len(CTX_LOADS))]
        s_ln = sem("s_ln")
        s_var = sem("s_var")
        s_std = sem("s_std")
        s_xn = sem("s_xn")
        s_xnT_ps = sem("s_xnT_ps")
        s_xnT = sem("s_xnT")
        s_q_ps = sem("s_q_ps")
        s_k_ps = sem("s_k_ps")
        s_v_ps = sem("s_v_ps")
        s_v_done = sem("s_v_done")
        s_p1 = sem("s_p1")
        s_r1 = sem("s_r1")
        s_p2 = sem("s_p2")
        s_p3 = sem("s_p3")
        s_kst = [sem(f"s_kst{i}") for i in range(KRING)]
        s_qsplit = sem("s_qsplit")
        s_qst = sem("s_qst")
        s_q_loaded = [sem(f"s_q_loaded{s}") for s in range(SQ // QH)]
        s_k_piece = [sem(f"s_k_piece{i}") for i in range(len(KEY_PIECES))]
        s_k_loaded = sem("s_k_loaded")
        s_wq = sem("s_wq")
        s_bo = sem("s_bo")
        s_rows = sem("s_rows")
        s_rows2 = sem("s_rows2")
        s_small = sem("s_small")
        s_zeros = sem("s_zeros")
        s_cleared = sem("s_cleared")
        s_w1 = [sem(f"s_w1_{i}") for i in range(RING)]
        s_w2 = [sem(f"s_w2_{i}") for i in range(RING)]
        s_vones = sem("s_vones")
        s_warm = sem("s_warm")
        s_minus_q = sem("s_minus_q")
        s_f_scores = sem("s_f_scores")
        s_f_above = sem("s_f_above")
        s_f_max = sem("s_f_max")
        s_f_seen = sem("s_f_seen")
        s_f_kept = sem("s_f_kept")
        s_a_scores = sem("s_a_scores")
        s_a_free = sem("s_a_free")
        s_b_scores = sem("s_b_scores")
        s_exp = sem("s_exp")
        s_pv = sem("s_pv")
        s_vst = sem("s_vst")
        s_acc_sb = sem("s_acc_sb")
        s_acc_T = sem("s_acc_T")
        s_recip = sem("s_recip")
        s_acc_free = sem("s_acc_free")
        s_mchain = sem("s_mchain")
        s_m_T = sem("s_m_T")
        s_m_rows = sem("s_m_rows")
        s_m_loaded = sem("s_m_loaded")

        MSTEPS = 5

        place = keys[:].bitcast(F32)
        W1C = 2 * H
        second = HG * SKP // 2
        w1_at = [i * W1C for i in range(RING)]
        w2_at = [(RING + i) * W1C if i < RING // 2 else second + (i - RING // 2) * W1C for i in range(RING)]
        assert (RING + RING // 2) * W1C <= second
        w1 = [place[:, o:o + W1C].rearrange("p (e h) -> p e h", e=2) for o in w1_at]
        w2 = [place[:, o:o + W1C].rearrange("p (e c d) -> p e c d", e=2, d=D) for o in w2_at]

        def load_w1(eng, p, slot):
            eng.dma_start(w1[slot], a["w1"][ds(2 * p, 2)].rearrange("e d h -> d e h")).then_inc(s_w1[slot], 16)

        def load_w2(eng, p, slot):
            eng.dma_start(w2[slot].rearrange("p e c d -> p e (c d)"),
                          a["w2"][ds(2 * p, 2)].rearrange("e (p c) d -> p e (c d)", c=HC)).then_inc(s_w2[slot], 16)

        pctx = ExitStack()
        with pctx:
            late = keys[:, HG * SKP:2 * HG * SKP]
            late32 = late.bitcast(F32)
            ctx_t = late32[:, 0:SKP]
            wk_t = late32[:, SKP:SKP + D]
            wv_t = late32[:, SKP + D:SKP + 2 * D]
            wq_t = late32[:, SKP + 2 * D:SKP + 3 * D]
            split_at = 2 * (SKP + 3 * D)
            k_split = [late[:, split_at + i * 3 * CW:split_at + (i + 1) * 3 * CW] for i in range(KRING)]
            q_split = late[:, split_at + KRING * 3 * CW:split_at + KRING * 3 * CW + 3 * SQ]
            k_rest = [probs[:, o:o + CW] for o in (0, CW, 2 * CW + 4 * SQ, 3 * CW + 4 * SQ)]
            q_full = probs[:, 2 * CW:2 * CW + SQ]
            minus_q = probs[:, 2 * CW + SQ:2 * CW + 2 * SQ].bitcast(BF16)[:, 0:HG * QH]
            above = [probs[:, 2 * CW + 2 * SQ + i * CW:2 * CW + 2 * SQ + i * CW + AW] for i in range(FBUF)]
            xn = probs[:, 2 * CW + SQ:2 * CW + 2 * SQ]
            xnT = probs[:, 2 * CW + 2 * SQ:2 * CW + 3 * SQ]

            block = pctx.enter_context(nc.Block())

            def width(c):
                return CW if c < NCHUNK - 1 else LASTW

            def first_query(t):
                return (t % 2) * (NH * QH) + (t // 2) * (HG * QH)

            @block.sync
            def _(sp):
                sp.dma_start(resid[:].rearrange("p (t d) -> p t d", d=D),
                             a["x"].rearrange("o (t p) d -> p (o t) d", p=P)).then_inc(s_x, 16)
                sp.dma_start(wk_t, a["wk_t"]).then_inc(s_w, 16)
                sp.dma_start(ident[:], a["c_ident"]).then_inc(s_consts, 16)
                sp.dma_start(wv_t, a["wv_t"]).then_inc(s_w, 16)
                for i, (c0, c1) in enumerate(CTX_LOADS):
                    k0, k1 = c0 * CW, min(c1 * CW, SKP)
                    sp.dma_start(ctx_t[:, k0:k1], a["ctx_t"][:, k0:k1]).then_inc(s_ctx[i], 16)
                    if i == 0:
                        sp.dma_start(wq_t, a["wq_t"]).then_inc(s_wq, 16)
                sp.dma_start(identb[:], a["c_identb"]).then_inc(s_constb, 16)

                def store_k(c):
                    w = width(c)
                    sp.wait_ge(s_p3, c + 1)
                    sp.dma_start(k_parts_d[:, :, c * CW:c * CW + w].rearrange("j p k -> p j k"),
                                 k_split[c % KRING].rearrange("p (j k) -> p j k", j=3)[:, :, 0:w]
                                 ).then_inc(s_kst[c % KRING], 16)

                def load_q(s):
                    sp.wait_ge(s_qst, 16)
                    for i in range(3):
                        src = q_parts_d[i, s].rearrange("(o d h) q -> o d (h q)", o=1, d=DK)
                        sp.dma_start(queries[i * 3 * DK:(i + 1) * 3 * DK, s * NH * QH:(s + 1) * NH * QH],
                                     src.broadcast_to([3, DK, NH * QH])).then_inc(s_q_loaded[s], 16)

                def load_piece(i):
                    (c0, c1), _ = KEY_PIECES[i]
                    for c in range(max(c0, c1 - KRING), c1):
                        sp.wait_ge(s_kst[c % KRING], 16 * (c // KRING + 1))
                    k0, k1 = c0 * CW, min(c1 * CW, SKP)
                    for r in range(3):
                        sp.dma_start(keys[r * 3 * DK:(r + 1) * 3 * DK, 0:HG * SKP]
                                     .rearrange("r (h k) -> r h k", h=HG)[:, :, k0:k1],
                                     k_parts_d.rearrange("j (d h) k -> (j d) h k", d=DK)[:, 0:HG, k0:k1]
                                     ).then_inc(s_k_piece[i], 16)

                def load_keys(hg):
                    b = (hg % 2) * HG * SKP
                    src = k_parts_d.rearrange("(o j) (d h) k -> o (j d) (h k)", o=1, d=DK)
                    sp.dma_start(keys[0:ROW_K, b:b + HG * SKP],
                                 src[:, :, hg * HG * SKP:(hg + 1) * HG * SKP]
                                 .broadcast_to([3, 3 * DK, HG * SKP])).then_inc(s_k_loaded, 16)

                for c in range(NCHUNK):
                    store_k(c)
                    if c == 1:
                        sp.wait_ge(s_qsplit, 4)
                        sp.dma_start(q_parts_d.rearrange("j s p q -> p (j s) q"),
                                     q_split.rearrange("p (n q) -> p n q", q=QH)).then_inc(s_qst, 16)
                    if c == 3:
                        load_q(0)
                    if c == KEY_PIECES[0][0][1]:
                        load_piece(0)
                for i in range(1, len(KEY_PIECES)):
                    load_piece(i)
                load_q(1)
                load_keys(1)

                def max_rows_of(t):
                    sp.wait_ge(s_m_rows, t + 1)
                    c = first_query(t)
                    sp.dma_start(queries[ROW_M:ROW_M + 3, c:c + HG * QH].rearrange("i (u q) -> i u q", q=P),
                                 max_rows[:]).then_inc(s_m_loaded, 16)

                for t in range(NG):
                    max_rows_of(t)
                    hg = t // 2 + 1
                    if t % 2 == 0 and t >= 2 and hg < NH // HG:
                        sp.wait_ge(s_pv, 2 * (hg - 1) * KT + 3)
                        load_keys(hg)
                    if t == NG - 2:
                        sp.wait_ge(s_pv, (NG - 2) * KT + 3)
                        for p in range(RING):
                            load_w1(sp, p, p)
                        for p in range(RING // 2):
                            load_w2(sp, p, p)

            @block.gpsimd
            def _(pool):
                pool.dma_start(bo_t[:], a["b_o"].rearrange("(o d) -> o d", o=1).broadcast_to([P, D])).then_inc(s_bo, 16)
                pool.dma_start(queries[ROW_K:96, :], a["c_queries"]).then_inc(s_rows, 16)
                for b in range(HG):
                    pool.dma_start(keys[ROW_K:96, b * SKP:(b + 1) * SKP], a["c_keys"]).then_inc(s_rows, 16)
                vals = values[:].rearrange("p (k h v) -> p k h v", h=NH, v=VW)
                pool.memset(vals[:, :, :, DK], 1.0).then_inc(s_vones, 1)
                pool.wait_ge(s_vones, 1)
                pool.memset(vstage[:], 0.0).then_inc(s_vones, 1)
                pool.wait_ge(s_vones, 2)
                pool.memset(queries[96:P, :].bitcast(F32), 0.0).then_inc(s_vones, 1)
                pool.wait_ge(s_vones, 3)
                pool.memset(keys[96:P, 0:HG * SKP].bitcast(F32), 0.0).then_inc(s_vones, 1)
                pool.wait_ge(s_vones, 4)
                pool.wait_ge(s_v_done, NCHUNK)
                pool.wait_ge(s_qst, 16)
                for c in range(NCHUNK - KRING, NCHUNK):
                    pool.wait_ge(s_kst[c % KRING], 16 * (c // KRING + 1))
                for b in range(HG, 2 * HG):
                    pool.dma_start(keys[ROW_K:96, b * SKP:(b + 1) * SKP], a["c_keys"]).then_inc(s_rows2, 16)
                pool.memset(keys[96:P, HG * SKP:2 * HG * SKP].bitcast(F32), 0.0).then_inc(s_vones, 1)
                pool.wait_ge(s_vones, 5)
                pool.memset(heads_out[:], 0.0).then_inc(s_zeros, 1)
                pool.wait_ge(s_zeros, 1)
                pool.memset(heads_out[:, D:D + 1], 1.0).then_inc(s_zeros, 1)
                pool.wait_ge(s_zeros, 2)
                pool.dma_start(x_slots_d.rearrange("(n p) d -> p n d", p=P),
                               heads_out[:, 0:D + 1].rearrange("p (o d) -> p o d", o=1)
                               .broadcast_to([P, E * CAP // P, D + 1])).then_inc(s_cleared, 16)
                pool.dma_start(y_tokens_d.rearrange("(n p) d -> p n d", p=P),
                               heads_out[:, 0:D].rearrange("p (o d) -> p o d", o=1)
                               .broadcast_to([P, SQ * TOPK // P, D])).then_inc(s_cleared, 16)
                for t, n in ((wo_t, "wo_t"), (gate_w, "gate_w"), (b1_t, "b1_t"), (b2_t, "b2"),
                             (experts, "c_experts"), (results, "c_results"), (before, "c_before"), (ones, "c_ones")):
                    pool.dma_start(t[:], a[n]).then_inc(s_small, 16)
                pool.dma_start(gate_b[:], a["gate_b"].rearrange("(o d) -> o d", o=1).broadcast_to([P, E])).then_inc(s_small, 16)
                with pool.Fori(0, NG) as t:
                    hg = pool.snap(t // 2)
                    with pool.Fori(0, IT) as it:
                        for j in range(3):
                            pool.wait_ge(s_pv, t * KT + it * 3 + j + 1)
                            pool.tensor_copy(
                                vstage[:, j * HG * 32:(j + 1) * HG * 32].rearrange("p (h v) -> p h v", v=32)[:, :, 0:VW],
                                values[:, ds(it * (3 * NH * VW) + hg * (HG * VW) + j * NH * VW, HG * VW)]
                                .rearrange("p (h v) -> p h v", v=VW)).then_inc(s_vst, 1)

            @block.scalar
            def _(act):
                act.wait_ge(s_var, 1)
                act.activation(stats[:, 8 * TILES:9 * TILES].rearrange("p (t o) -> p t o", o=1),
                               stats[:, 6 * TILES:8 * TILES].rearrange("p (t m) -> p t m", m=2)[:, :, 1:2],
                               ACT.Sqrt, bias=eps_t[:, 0:1]).then_inc(s_std, 1)
                vals = values[:].rearrange("p (k h v) -> p k h v", h=NH, v=VW)
                act.wait_ge(s_vones, 1)

                def first_part(c):
                    w, i = width(c), c % 2
                    act.wait_ge(s_k_ps, c + 1)
                    if c >= KRING:
                        act.wait_ge(s_kst[c % KRING], 16 * (c // KRING))
                    act.activation(k_split[c % KRING][:, 0:w], bank(4 + i, w), ACT.Copy).then_inc(s_p1, 1)

                def second_part(c):
                    w = width(c)
                    act.wait_ge(s_r1, c + 1)
                    act.activation(k_split[c % KRING][:, CW:CW + w], k_rest[c % 4][:, 0:w], ACT.Copy).then_inc(s_p2, 1)

                first_part(0)
                for c in range(NCHUNK):
                    w = width(c)
                    act.wait_ge(s_v_ps, c + 1)
                    act.activation(vals[:, c * 4:c * 4 + w // P, :, 0:DK],
                                   bank(6 + c % 2, w).rearrange("p (k h d) -> p k h d", h=NH, d=DK),
                                   ACT.Copy).then_inc(s_v_done, 1)
                    if c + 1 < NCHUNK:
                        first_part(c + 1)
                    second_part(c)
                act.activation(warm[:], eps_t[:], ACT.Exp).then_inc(s_warm, 1)
                act.wait_ge(s_qsplit, 4)
                with act.Fori(0, ACH // 2) as n:
                    for u in range(UNITS):
                        act.wait_ge(s_f_max, n * UNITS + u + 1)
                        act.wait_ge(s_f_scores, n * UNITS + u + 1)
                        act.activation(above[u % FBUF], bank(2 * (u % FBUF) + 1, AW), ACT.Relu).then_inc(s_f_above, 1)
                act.sem_inc(s_exp, 3)

                def copy_sums(t):
                    act.wait_ge(s_pv, (t + 1) * KT + 3)
                    act.activation(acc_copy[:], bank(7), ACT.Copy).then_inc(s_acc_sb, 1)

                def exps(t, it, banks, before=None):
                    for j in range(3):
                        if before is not None and j == 1:
                            copy_sums(before)
                        act.wait_ge(s_pv, t * KT + it * 3 + j + 1)
                        for h in range(HG):
                            n = j * HG + h
                            act.wait_ge(s_b_scores, t * (KT * HG) + it * (3 * HG) + n + 1)
                            act.activation(probs[:, n * QH:(n + 1) * QH], bank(banks[n % len(banks)]),
                                           ACT.Exp).then_inc(s_exp, 1)

                def group(t, banks, before=None):
                    exps(t, 0, banks, before)
                    with act.Fori(0, (IT - 1) // TURN_ALONE) as n:
                        for k in range(TURN_ALONE):
                            exps(t, n * TURN_ALONE + (k + 1), banks)

                group(0, BANKS)
                with act.Fori(1, NG - 1) as t:
                    group(t, BANKS, t - 1)
                group(NG - 1, LAST_BANKS, NG - 2)
                copy_sums(NG - 1)

            @block.vector
            def _(dve):
                count = [0]

                def link(ins):
                    count[0] += 1
                    ins.then_inc(s_ln, 1)
                    dve.wait_ge(s_ln, count[0])

                link(dve.memset(eps_t[:], EPS))
                link(dve.memset(max_parts[:], 0.0))
                link(dve.memset(chunk_max[:, ACH // 2 * UNITS:], -3.0e38))
                dve.wait_ge(s_x, 16)
                layer_norm(dve, link, resid[:], xn, stats, s_var, s_std, 1, s_xn)

                def rest_k(c):
                    w, i = width(c), c % 2
                    dve.wait_ge(s_p1, c + 1)
                    dve.tensor_tensor(k_rest[c % 4][:, 0:w], bank(4 + i, w), k_split[c % KRING][:, 0:w],
                                      ALU.subtract).then_inc(s_r1, 1)

                def last_k(c):
                    w, i = width(c), c % 2
                    p = k_split[c % KRING]
                    dve.wait_ge(s_p2, c + 1)
                    dve.tensor_tensor(p[:, 2 * CW:2 * CW + w], k_rest[c % 4][:, 0:w], p[:, CW:CW + w],
                                      ALU.subtract).then_inc(s_p3, 1)

                dve.wait_ge(s_xnT_ps, 1)
                for i in range(2):
                    dve.tensor_copy(xnT[:, i * 512:(i + 1) * 512], bank(i)).then_inc(s_xnT, 1)
                rest_k(0)
                dve.wait_ge(s_q_ps, 2)
                for i in range(2):
                    link(dve.tensor_scalar(q_full[:, i * 512:(i + 1) * 512], bank(2 + i), float(1.0 / np.sqrt(DK)),
                                           None, ALU.mult))
                dve.tensor_copy(q_split[:, 0:SQ], q_full).then_inc(s_qsplit, 1)
                dve.wait_ge(s_qsplit, 1)
                link(dve.tensor_tensor(q_full, q_full, q_split[:, 0:SQ], ALU.subtract))
                dve.tensor_copy(q_split[:, SQ:2 * SQ], q_full).then_inc(s_qsplit, 1)
                dve.wait_ge(s_qsplit, 2)
                dve.tensor_tensor(q_split[:, 2 * SQ:3 * SQ], q_full, q_split[:, SQ:2 * SQ],
                                  ALU.subtract).then_inc(s_qsplit, 2)
                for c in range(NCHUNK):
                    if c + 1 < NCHUNK:
                        rest_k(c + 1)
                    last_k(c)
                    if c == NCHUNK - 2:
                        dve.wait_ge(s_rows, 16 * 5)
                        dve.wait_ge(s_vones, 4)
                        dve.wait_ge(s_q_loaded[0], 16 * 3)
                        dve.tensor_scalar(minus_q, queries[:, 0:HG * QH], -1.0, None, ALU.mult).then_inc(s_minus_q, 1)


                dve.sem_inc(s_f_max, FBUF)
                dve.sem_inc(s_acc_free, 1)

                def pass_a(t, it, before=None):
                    for p in range(UNITS // 2):
                        if before is not None and p == BEFORE_T:
                            normalise(before)
                        dve.wait_ge(s_a_scores, (t - 1) * (ACH * UNITS // 2) + it * (UNITS // 2) + p + 1)
                        src = psum[:, (p % 2) * 1024:(p % 2) * 1024 + 1024].rearrange("q (b k) -> q b k", b=2)
                        dve.tensor_reduce(chunk_max[:, ds(it * UNITS + 2 * p, 2)], src[:, :, 0:AW],
                                          AX.X, ALU.max).then_inc(s_a_free, 1)

                def max_chain(t):
                    base = t * MSTEPS
                    if isinstance(t, int) and t == 0:
                        dve.wait_ge(s_f_max, ACH // 2 * UNITS + FBUF)
                    else:
                        dve.wait_ge(s_a_free, t * (ACH * UNITS // 2) + 2)
                    dve.tensor_reduce(neg_max[:], chunk_max[:].rearrange("q (c u) -> q u c", u=UNITS),
                                      AX.X, ALU.max, negate=True).then_inc(s_mchain, 1)
                    dve.wait_ge(s_mchain, base + 1)
                    dve.tensor_copy(max_parts[:, 0:UNITS], neg_max[:]).then_inc(s_mchain, 1)
                    dve.wait_ge(s_mchain, base + 2)
                    dve.tensor_tensor(max_rest[:], neg_max[:], max_parts[:, 0:UNITS], ALU.subtract).then_inc(s_mchain, 1)
                    dve.wait_ge(s_mchain, base + 3)
                    dve.tensor_copy(max_parts[:, UNITS:2 * UNITS], max_rest[:]).then_inc(s_mchain, 1)
                    dve.wait_ge(s_mchain, base + 4)
                    dve.tensor_tensor(max_parts[:, 2 * UNITS:3 * UNITS], max_rest[:], max_parts[:, UNITS:2 * UNITS],
                                      ALU.subtract).then_inc(s_mchain, 1)
                    dve.wait_ge(s_m_T, t + 1)
                    if not isinstance(t, int) or t:
                        dve.wait_ge(s_m_loaded, t * 16)
                    dve.tensor_copy(max_rows[:], bank(0).bitcast(BF16)[0:3 * UNITS, 0:P]).then_inc(s_m_rows, 1)

                def normalise(t):
                    ps = bank(7).rearrange("q (t h v) -> q t h v", t=QT, v=32)
                    g, s = t // 2, t % 2
                    if not isinstance(t, int):
                        g, s = dve.snap(g), dve.snap(s)
                    dve.wait_ge(s_acc_T, t + 1)
                    dve.reciprocal(recip[:].rearrange("q (t h) -> q t h", t=QT), ps[:, :, :, DK]).then_inc(s_recip, 1)
                    dve.wait_ge(s_recip, t + 1)
                    dve.tensor_tensor(
                        heads_out[:].rearrange("q (s t g h d) -> q g s t h d", s=SQ // QH, t=QT, g=NH // HG, d=DK)[:, g, s],
                        ps[:, :, :, 0:DK],
                        recip[:].rearrange("q (t h o) -> q t h o", t=QT, o=1).broadcast_to([P, QT, HG, DK]),
                        ALU.mult).then_inc(s_acc_free, 1)

                def group(t, before=None):
                    pass_a(t, 0, before)
                    with dve.Fori(0, (ACH - 1) // PER_TURN) as n:
                        for k in range(PER_TURN):
                            pass_a(t, n * PER_TURN + (k + 1))
                    max_chain(t)

                with dve.Fori(0, ACH // 2) as n:
                    for u in range(UNITS):
                        dve.wait_ge(s_f_above, n * UNITS + u + 1)
                        dve.sem_inc(s_f_seen, 1)
                        dve.tensor_tensor_reduce(out=above[u % FBUF], in0=bank(2 * (u % FBUF), AW), in1=above[u % FBUF],
                                                 scale=1.0, scalar=-3.0e38, op0=ALU.add, op1=ALU.max,
                                                 accum_out=pair_max[:, u:u + 1]).then_inc(s_f_max, 1)
                    dve.wait_ge(s_f_max, n * UNITS + (UNITS + FBUF))
                    dve.tensor_copy(chunk_max[:, ds(n * UNITS, UNITS)], pair_max[:]).then_inc(s_f_kept, 1)
                    dve.wait_ge(s_f_kept, n + 1)
                dve.sem_inc(s_a_free, 2)
                max_chain(0)
                dve.wait_ge(s_bo, 16)
                link(dve.tensor_tensor(resid[:].rearrange("p (t d) -> p t d", d=D), resid[:].rearrange("p (t d) -> p t d", d=D),
                                       bo_t[:].rearrange("p (o d) -> p o d", o=1).broadcast_to([P, TILES, D]), ALU.add))
                group(1)
                dve.wait_ge(s_cleared, 32)
                with dve.Fori(2, NG) as t:
                    group(t, before=t - 2)
                normalise(NG - 2)
                normalise(NG - 1)

            @block.tensor
            def _(pe):

                def project(c):
                    w, i = width(c), c % 2
                    for n, (c0, _) in enumerate(CTX_LOADS):
                        if c == c0:
                            pe.wait_ge(s_ctx[n], 16)
                            if n == 0:
                                pe.wait_ge(s_w, 32)
                    if c >= 2:
                        pe.wait_ge(s_r1, c - 1)
                    pe.matmul(bank(4 + i, w), wk_t, ctx_t[:, c * CW:c * CW + w], start=True, stop=True).then_inc(s_k_ps, 1)
                    if c >= 2:
                        pe.wait_ge(s_v_done, c - 1)
                    for k in range(w // P):
                        v = pe.matmul(bank(6 + i, P, k * P), ctx_t[:, c * CW + k * P:c * CW + (k + 1) * P], wv_t,
                                      start=True, stop=True)
                    v.then_inc(s_v_ps, 1)

                pe.wait_ge(s_consts, 16)
                pe.wait_ge(s_xn, 1)
                for k in range(TILES):
                    v = pe.transpose(bank(k // 4, P, (k % 4) * P), xn[:, k * P:(k + 1) * P], ident[:])
                v.then_inc(s_xnT_ps, 1)
                project(0)
                pe.wait_ge(s_wq, 16)
                for k in range(2):
                    pe.wait_ge(s_xnT, k + 1)
                    pe.matmul(bank(2 + k), wq_t, xnT[:, k * 512:(k + 1) * 512], start=True, stop=True).then_inc(s_q_ps, 1)
                for c in range(1, NCHUNK):
                    project(c)
                pe.wait_ge(s_r1, NCHUNK)
                pe.wait_ge(s_v_done, NCHUNK)
                pe.sem_inc(s_pv, 3)
                pe.sem_inc(s_k_loaded, 16)

                def a_pair(t, qa, it, kbuf, p):
                    pe.wait_ge(s_a_free, (t - 1) * (ACH * UNITS // 2) + it * (UNITS // 2) + p + 1)
                    for k in range(2):
                        u = 2 * p + k
                        m = pe.matmul(bank((p % 2) * 2 + k, AW),
                                      queries[:, ds(qa + u * P, P)],
                                      keys[:, ds(kbuf * (HG * SKP) + it * AW + (u // QT) * SKP, AW)],
                                      start=True, stop=True)
                    m.then_inc(s_a_scores, 1)

                def first_pair(n, u):
                    pe.wait_ge(s_f_max, n * UNITS + u + 1)
                    q = queries[:, u * P:(u + 1) * P]
                    ka, kb = (keys[:, ds(n * (2 * AW) + (u // QT) * SKP + k * AW, AW)] for k in range(2))
                    a_bank, diff_bank = (bank(2 * (u % FBUF) + k, AW) for k in range(2))
                    pe.matmul(a_bank, q, ka, start=True, stop=True)
                    pe.matmul(diff_bank, q, kb, start=True, stop=False)
                    pe.matmul(diff_bank, minus_q[:, u * P:(u + 1) * P], ka, start=False, stop=True).then_inc(s_f_scores, 1)

                def b_scores(t, qb, it, kbuf, n, banks, first):
                    j, h = n // HG, n % HG
                    if first and n < 3:
                        more = 0
                    elif first and n < len(banks):
                        more = n - 2
                    else:
                        more = len(banks) - 3
                    pe.wait_ge(s_exp, t * (KT * HG) + it * (3 * HG) + n + 1 - more)
                    pe.matmul(bank(banks[n % len(banks)]),
                              keys[:, ds(kbuf * (HG * SKP) + it * (3 * P) + h * SKP + j * P, P)],
                              queries[:, ds(qb + h * QH, QH)],
                              start=True, stop=True).then_inc(s_b_scores, 1)

                def pv(t, it, j, first=False, last=False):
                    pe.wait_ge(s_exp, t * (KT * HG) + it * (3 * HG) + (j + 1) * HG + 3)
                    pe.wait_ge(s_vst, t * KT + it * 3 + j + 1)
                    if first:
                        pe.wait_ge(s_acc_free, t + 1)
                    for h in range(HG):
                        m = pe.matmul(psum[h * 32:(h + 1) * 32, 7 * 512:8 * 512],
                                      vstage[:, (j * HG + h) * 32:(j * HG + h + 1) * 32],
                                      probs[:, (j * HG + h) * QH:(j * HG + h + 1) * QH],
                                      start=first, stop=last)
                    m.then_inc(s_pv, 1)

                def max_transpose(t):
                    pe.wait_ge(s_mchain, t * MSTEPS + 5)
                    pe.transpose(bank(0).bitcast(BF16)[:, 0:P], max_parts[:], identb[:]).then_inc(s_m_T, 1)

                def both(ta, tb, it, kba, kbb, qa, qb, first=False, before=None, a=True, chain=False,
                         banks=BANKS):
                    done = {"S": 0, "A": 0, "V": 0}
                    orders = (HEAD, HEAD_ALONE) if first else (ORDER, TAIL if chain else ALONE)
                    for step in orders[0 if a else 1]:
                        if step == "M":
                            max_transpose(ta)
                            continue
                        if step == "T":
                            if before is not None:
                                acc_transposes(before)
                            continue
                        n = done[step]
                        done[step] += 1
                        if step == "S":
                            b_scores(tb, qb, it, kbb, n, banks, first)
                        elif step == "A":
                            a_pair(ta, qa, it, kba, n)
                        elif n:
                            pv(tb, it, n - 1, first=first and n == 1)
                        elif not first:
                            pv(tb, it - 1, 2)
                        elif before is not None:
                            finish(before)

                def finish(t):
                    pv(t, IT - 1, 2, last=True)

                def acc_transposes(t):
                    pe.wait_ge(s_acc_sb, t + 1)
                    for k in range(QT):
                        m = pe.transpose(bank(7, P, k * P), acc_copy[:, k * P:(k + 1) * P], ident[:])
                    m.then_inc(s_acc_T, 1)

                pe.wait_ge(s_rows, 16 * 5)
                pe.wait_ge(s_vones, 4)
                pe.wait_ge(s_q_loaded[0], 16 * 3)
                pe.wait_ge(s_minus_q, 1)
                for i, (_, (n0, n1)) in enumerate(KEY_PIECES):
                    pe.wait_ge(s_k_piece[i], 16 * 3)
                    with pe.Fori(n0, n1) as n:
                        for u in range(UNITS):
                            first_pair(n, u)
                pe.wait_ge(s_constb, 16)
                max_transpose(0)
                pe.wait_ge(s_q_loaded[1], 16 * 3)
                pe.wait_ge(s_rows2, 16 * 4)
                pe.wait_ge(s_vones, 5)

                def columns(t):
                    buf, q = (t // 2) % 2, first_query(t)
                    return (buf, q) if isinstance(t, int) else (pe.snap(buf), pe.snap(q))

                def head(ta, before=None):
                    (kba, qa), (kbb, qb) = columns(ta), columns(ta - 1)
                    pe.wait_ge(s_k_loaded, (ta // 2 + 1) * 16)
                    pe.wait_ge(s_m_loaded, ta * 16)
                    both(ta, ta - 1, 0, kba, kbb, qa, qb, first=True, before=before)

                def rest(ta):
                    (kba, qa), (kbb, qb) = columns(ta), columns(ta - 1)
                    with pe.Fori(0, (ACH - 1) // PER_TURN) as n:
                        for k in range(PER_TURN):
                            both(ta, ta - 1, n * PER_TURN + (k + 1), kba, kbb, qa, qb)
                    both(ta, ta - 1, ACH, kba, kbb, qa, qb, a=False, chain=True)

                head(1)
                with pe.Fori(1, NG - 1) as ta:
                    rest(ta)
                    head(ta + 1, before=ta - 1)
                rest(NG - 1)
                tb = NG - 1
                kbb, qb = columns(tb)
                pe.wait_ge(s_m_loaded, NG * 16)
                both(0, tb, 0, 0, kbb, 0, qb, first=True, before=tb - 1, a=False, banks=LAST_BANKS)
                with pe.Fori(0, (IT - 1) // TURN_ALONE) as n:
                    for k in range(TURN_ALONE):
                        both(0, tb, n * TURN_ALONE + (k + 1), 0, kbb, 0, qb, a=False, banks=LAST_BANKS)
                finish(tb)
                acc_transposes(tb)


        at = [second + (RING // 2) * W1C]

        def carve(n):
            at[0] += n
            assert at[0] <= 2 * second
            return place[:, at[0] - n:at[0]]

        x_in = [carve(D + 1) for _ in range(RING)]
        y_out = [carve(D) for _ in range(RING)]
        xT = [carve(P) for _ in range(2)]
        h_rows = [carve(H) for _ in range(2)]
        h_cols = [carve(H) for _ in range(2)]
        h_gelu = [carve(H) for _ in range(2)]
        y_got = carve(TOPK * TILES * D)

        val = values[:]
        heads_T, xf, xfT, work3 = (val[:, i * 1024:(i + 1) * 1024] for i in range(4))
        logits = val[:, 4096:4608]
        work = val[:, 4608:5120]
        works = [work, work3[:, 0:512], work3[:, 512:1024]]
        prb = probs[:]
        chosen = [prb[:, k * 512:(k + 1) * 512] for k in range(TOPK)]
        weights = prb[:, 1536:2048]
        weights_T = prb[0:E, 2048:3072]
        qry = queries[:].bitcast(F32)
        top8 = qry[:, 0:64]
        expert_f = qry[:, 64:88]
        gates = qry[:, 88:112]
        place_f = qry[:, 112:136]
        slot_f = qry[:, 136:160]
        over = qry[:, 160:184]
        gsum = qry[:, 184:192]
        none_before = (TILES - 1) * E
        counts_pad = queries[:, 1024:1024 + none_before + TILES * E]
        counts = counts_pad[:, none_before:]
        idx8 = queries[:, 2048:2176].bitcast(U32)
        to_slot = queries[:, 2176:2176 + 48].bitcast(U32)
        xk = [qry[:, 1280 + k * TILES * (D + 1):1280 + (k + 1) * TILES * (D + 1)] for k in range(TOPK)]

        s_hT = sem("s_hT")
        s_hT_sb = sem("s_hT_sb")
        s_proj = sem("s_proj")
        s_c = sem("s_c")
        s_var2 = sem("s_var2")
        s_std2 = sem("s_std2")
        s_xf = sem("s_xf")
        s_xfT = sem("s_xfT")
        s_xfT_sb = sem("s_xfT_sb")
        s_logits = sem("s_logits")
        s_top = sem("s_top")
        s_expg = sem("s_expg")
        s_counts = sem("s_counts")
        s_prefix = sem("s_prefix")
        s_slots = sem("s_slots")
        s_sent = sem("s_sent")
        s_wts = sem("s_wts")
        s_wts_T = sem("s_wts_T")
        s_wts_sb = sem("s_wts_sb")
        s_b2 = sem("s_b2")
        s_b2_added = sem("s_b2_added")
        s_xin = [sem(f"s_xin{i}") for i in range(RING)]
        s_yst = [sem(f"s_yst{i}") for i in range(RING)]
        s_xT_ps = sem("s_xT_ps")
        s_xT = sem("s_xT")
        s_h_ps = sem("s_h_ps")
        s_h = sem("s_h")
        s_hc_ps = sem("s_hc_ps")
        s_hc = sem("s_hc")
        s_gelu = sem("s_gelu")
        s_y_ps = sem("s_y_ps")
        s_y = sem("s_y")
        s_got = [sem(f"s_got{i}") for i in range(TILES // 2)]
        s_xk = sem("s_xk")
        s_y_seen = sem("s_y_seen")
        s_sum = sem("s_sum")
        s_out = sem("s_out")
        STEPS = PAIRS + 3

        def pipeline(eng, stages):
            def step(turn, u):
                for lag, stage in stages:
                    p = turn * RING + (u - lag)
                    if not isinstance(p, int) or 0 <= p < PAIRS:
                        stage(p, (u - lag) % RING, turn + (u - lag) // RING)

            for u in range(RING):
                step(0, u)
            with eng.Fori(1, PAIRS // RING) as turn:
                for u in range(RING):
                    step(turn, u)
            for u in range(STEPS - PAIRS):
                step(PAIRS // RING, u)

        def reached(eng, s, n):
            if not isinstance(n, int) or n > 0:
                eng.wait_ge(s, n)

        with nc.Block() as block:

            @block.sync
            def _(sp):
                for p in range(RING // 2, RING):
                    load_w2(sp, p, p)
                sp.wait_ge(s_sent, 16 * TOPK * TILES)

                def load_x(p, slot):
                    sp.dma_start(x_in[slot], x_slots_d[ds(p * P, P), :]).then_inc(s_xin[slot], 16)

                for p in range(RING):
                    load_x(p, p)
                with sp.Fori(0, PAIRS // RING - 1) as n:
                    for u in range(RING):
                        p = n * RING + u
                        sp.wait_ge(s_y, p + 1)
                        load_w1(sp, p + RING, u)
                        load_w2(sp, p + RING, u)
                        if u:
                            sp.wait_ge(s_yst[u - 1], n * 16 + 16)
                            load_x(p + (RING - 1), u - 1)
                    sp.wait_ge(s_yst[RING - 1], n * 16 + 16)
                    load_x(n * RING + (2 * RING - 1), RING - 1)
                for u in range(RING):
                    sp.wait_ge(s_yst[u], 16 * (PAIRS // RING))
                for i in range(TILES // 2):
                    n = 2 * TOPK
                    sp.dma_start(y_got[:, i * n * D:(i + 1) * n * D].rearrange("p (n d) -> p n d", d=D),
                                 y_tokens_d[i * n * P:(i + 1) * n * P].rearrange("(n p) d -> p n d", p=P)
                                 ).then_inc(s_got[i], 16)
                for i in range(2):
                    h = TILES // 2
                    sp.wait_ge(s_sum, (i + 1) * h * TOPK)
                    sp.dma_start(out.rearrange("o (t p) d -> p (o t) d", p=P)[:, i * h:(i + 1) * h],
                                 resid[:, i * h * D:(i + 1) * h * D].rearrange("p (t d) -> p t d", d=D)
                                 ).then_inc(s_out, 16)
                sp.wait_ge(s_out, 32)

            @block.gpsimd
            def _(pool):
                pool.wait_ge(s_cleared, 32)
                pool.wait_ge(s_xk, TOPK + 1)
                pool.wait_ge(s_slots, 1)
                for t in range(TILES):
                    for k in range(TOPK):
                        c = k * TILES + t
                        pool.indirect_dma_start(
                            out=x_slots_d, out_offset=bass.IndirectOffsetOnAxis(ap=to_slot[:, c:c + 1], axis=0),
                            in_=xk[k][:, t * (D + 1):(t + 1) * (D + 1)], in_offset=None,
                            bounds_check=E * CAP - 1, oob_is_err=False).then_inc(s_sent, 16)

                def send_y(p, slot, turn):
                    pool.wait_ge(s_y, p + 1)
                    pool.sem_inc(s_y_seen, 1)
                    pool.indirect_dma_start(
                        out=y_tokens_d,
                        out_offset=bass.IndirectOffsetOnAxis(ap=x_in[slot][:, D:D + 1].bitcast(U32), axis=0),
                        in_=y_out[slot], in_offset=None,
                        bounds_check=SQ * TOPK - 1, oob_is_err=False).then_inc(s_yst[slot], 16)

                pipeline(pool, [(3, send_y)])

            @block.scalar
            def _(act):
                for i in range(2):
                    act.wait_ge(s_hT, i + 1)
                    act.activation(heads_T[:, i * 512:(i + 1) * 512], bank(i), ACT.Copy).then_inc(s_hT_sb, 1)
                act.wait_ge(s_var2, 1)
                act.activation(stats[:, 8 * TILES:9 * TILES].rearrange("p (t o) -> p t o", o=1),
                               stats[:, 6 * TILES:8 * TILES].rearrange("p (t m) -> p t m", m=2)[:, :, 1:2],
                               ACT.Sqrt, bias=eps_t[:, 0:1]).then_inc(s_std2, 1)
                act.wait_ge(s_xf, 1)
                for k in range(TOPK):
                    act.activation(xk[k].rearrange("p (t d) -> p t d", d=D + 1)[:, :, 0:D],
                                   xf.rearrange("p (t d) -> p t d", d=D), ACT.Copy).then_inc(s_xk, 1)
                for i in range(2):
                    act.wait_ge(s_xfT, i + 1)
                    act.activation(xfT[:, i * 512:(i + 1) * 512], bank(4 + i), ACT.Copy).then_inc(s_xfT_sb, 1)
                act.wait_ge(s_top, 1)
                act.activation(gates, gates, ACT.Exp).then_inc(s_expg, 1)
                act.activation(warm[:], eps_t[:], ACT.Gelu).then_inc(s_warm, 1)

                def copy_h(p, slot, turn):
                    act.wait_ge(s_h_ps, p + 1)
                    reached(act, s_hc_ps, p - 1)
                    act.activation(h_rows[slot % 2], bank(2 + slot % 2), ACT.Copy).then_inc(s_h, 1)

                def gelu(p, slot, turn):
                    act.wait_ge(s_hc, p + 1)
                    reached(act, s_y_ps, p - 1)
                    act.activation(h_gelu[slot % 2], h_cols[slot % 2], ACT.Gelu).then_inc(s_gelu, 1)

                pipeline(act, [(1, copy_h), (2, gelu)])

            @block.vector
            def _(dve):
                count = [0]

                def link(ins):
                    count[0] += 1
                    ins.then_inc(s_c, 1)
                    dve.wait_ge(s_c, count[0])

                def by_tile(t, n):
                    return t.rearrange("p (t n) -> p t n", n=n)

                def spread(t, n):
                    return t.rearrange("p (t o) -> p t o", o=1).broadcast_to([P, t.shape[1], n])

                dve.wait_ge(s_small, 16 * 9)
                link(dve.memset(counts_pad[:, 0:none_before], 0.0))
                for k in range(TOPK):
                    ins = dve.tensor_copy(xk[k].bitcast(U32).rearrange("p (t d) -> p t d", d=D + 1)[:, :, D:D + 1],
                                          results[:, k * TILES:(k + 1) * TILES].rearrange("p (t o) -> p t o", o=1))
                ins.then_inc(s_xk, 1)
                for i in range(2):
                    dve.wait_ge(s_proj, i + 1)
                    r = resid[:, i * 512:(i + 1) * 512]
                    link(dve.tensor_tensor(r, r, bank(2 + i), ALU.add))
                layer_norm(dve, link, resid[:], xf, stats, s_var2, s_std2, 1, s_xf)
                dve.wait_ge(s_logits, 1)
                link(dve.tensor_tensor(by_tile(logits, E), by_tile(bank(6), E),
                                       gate_b[:].rearrange("p (o e) -> p o e", o=1).broadcast_to([P, TILES, E]), ALU.add))
                for t in range(TILES):
                    ins = dve.max(top8[:, t * 8:(t + 1) * 8], logits[:, t * E:(t + 1) * E])
                link(ins)
                for t in range(TILES):
                    ins = dve.max_index(idx8[:, t * 8:(t + 1) * 8], top8[:, t * 8:(t + 1) * 8],
                                        logits[:, t * E:(t + 1) * E])
                link(ins)
                best = top8.rearrange("p (t k) -> p k t", k=8)
                by_k = gates.rearrange("p (k t) -> p k t", t=TILES)
                dve.tensor_tensor(by_k, best[:, 0:TOPK, :], best[:, 0:1, :].broadcast_to([P, TOPK, TILES]),
                                  ALU.subtract).then_inc(s_top, 1)
                link(dve.tensor_copy(expert_f.rearrange("p (k t) -> p k t", t=TILES),
                                     idx8.rearrange("p (t k) -> p k t", k=8)[:, 0:TOPK, :]))
                for k in range(TOPK):
                    ins = dve.tensor_tensor(by_tile(chosen[k], E),
                                            experts[:].rearrange("p (o e) -> p o e", o=1).broadcast_to([P, TILES, E]),
                                            spread(expert_f[:, k * TILES:(k + 1) * TILES], E), ALU.is_equal)
                link(ins)
                link(dve.tensor_tensor(work, chosen[0], chosen[1], ALU.add))
                dve.tensor_tensor(counts, work, chosen[2], ALU.add).then_inc(s_counts, 1)
                dve.wait_ge(s_expg, 1)
                link(dve.tensor_reduce(gsum, gates.rearrange("p (k t) -> p t k", t=TILES), AX.X, ALU.add))
                link(dve.reciprocal(gsum, gsum))
                link(dve.tensor_tensor(by_k, by_k, gsum.rearrange("p (o t) -> p o t", o=1)
                                       .broadcast_to([P, TOPK, TILES]), ALU.mult))
                dve.wait_ge(s_prefix, 1)
                for k in range(TOPK):
                    ins = dve.tensor_tensor(works[k], bank(7), chosen[k], ALU.mult)
                link(ins)
                for k in range(TOPK):
                    ins = dve.tensor_reduce(place_f[:, k * TILES:(k + 1) * TILES], by_tile(works[k], E), AX.X, ALU.add)
                link(ins)
                link(dve.tensor_scalar(over, place_f, float(CAP), None, ALU.is_ge))
                link(dve.tensor_scalar(slot_f, expert_f, float(CAP), None, ALU.mult))
                link(dve.scalar_tensor_tensor(slot_f, over, float(E * CAP), slot_f, ALU.mult, ALU.add))
                dve.tensor_tensor(to_slot, slot_f, place_f, ALU.add).then_inc(s_slots, 1)
                link(dve.tensor_scalar(over, over, -1.0, 1.0, ALU.mult, ALU.add))
                link(dve.tensor_tensor(gates, gates, over, ALU.mult))
                for k in range(TOPK):
                    dst = weights if k == 0 else work
                    link(dve.tensor_tensor(by_tile(dst, E), by_tile(chosen[k], E),
                                           spread(gates[:, k * TILES:(k + 1) * TILES], E), ALU.mult))
                    if k:
                        link(dve.tensor_tensor(weights, weights, work, ALU.add))
                dve.sem_inc(s_wts, 1)
                for i in range(2):
                    dve.wait_ge(s_wts_T, i + 1)
                    dve.tensor_copy(weights_T[:, i * 512:(i + 1) * 512], bank(4 + i)[0:E, :]).then_inc(s_wts_sb, 1)
                for i in range(2):
                    dve.wait_ge(s_b2, i + 1)
                    r = resid[:, i * 512:(i + 1) * 512]
                    dve.tensor_tensor(r, r, bank(2 + i), ALU.add).then_inc(s_b2_added, 1)

                def copy_x(p, slot, turn):
                    dve.wait_ge(s_xT_ps, p + 1)
                    reached(dve, s_h_ps, p - 1)
                    dve.tensor_copy(xT[slot % 2], bank(slot % 2, P)).then_inc(s_xT, 1)

                def bias(p, slot, turn):
                    dve.wait_ge(s_hc_ps, p + 1)
                    reached(dve, s_gelu, p - 1)
                    dve.tensor_tensor(
                        h_cols[slot % 2].rearrange("h (c e s) -> h c e s", c=HC, e=2),
                        bank(4 + slot % 2).rearrange("h (c e s) -> h c e s", c=HC, e=2),
                        b1_t[:, ds(p * (2 * HC), 2 * HC)].rearrange("h (e c o) -> h c e o", e=2, o=1)
                        .broadcast_to([P, HC, 2, CAP]), ALU.add).then_inc(s_hc, 1)

                def copy_y(p, slot, turn):
                    dve.wait_ge(s_y_ps, p + 1)
                    reached(dve, s_yst[slot], turn * 16)
                    dve.tensor_copy(y_out[slot], bank(6 + slot % 2, D)).then_inc(s_y, 1)

                pipeline(dve, [(0, copy_x), (2, bias), (3, copy_y)])
                dve.wait_ge(s_b2_added, 2)
                done = 0
                for i in range(TILES // 2):
                    dve.wait_ge(s_got[i], 16)
                    for k in range(TOPK):
                        for t in (2 * i, 2 * i + 1):
                            c, n = k * TILES + t, t * TOPK + k
                            r = resid[:, t * D:(t + 1) * D]
                            if k:
                                dve.wait_ge(s_sum, done - 1)
                            dve.scalar_tensor_tensor(r, y_got[:, n * D:(n + 1) * D], gates[:, c:c + 1], r,
                                                     ALU.mult, ALU.add).then_inc(s_sum, 1)
                            done += 1

            @block.tensor
            def _(pe):
                for i in range(2):
                    for k in range(4):
                        m = pe.transpose(bank(i, P, k * P), heads_out[:, (i * 4 + k) * D:(i * 4 + k + 1) * D], ident[:])
                    m.then_inc(s_hT, 1)
                pe.wait_ge(s_small, 16 * 9)
                for i in range(2):
                    pe.wait_ge(s_hT_sb, i + 1)
                    for k in range(4):
                        m = pe.matmul(bank(2 + i, D, k * D), heads_T[:, (i * 4 + k) * P:(i * 4 + k + 1) * P], wo_t[:],
                                      start=True, stop=True)
                    m.then_inc(s_proj, 1)
                pe.wait_ge(s_xf, 1)
                for i in range(2):
                    for k in range(4):
                        t = i * 4 + k
                        m = pe.transpose(bank(4 + i, P, k * P), xf[:, t * D:(t + 1) * D], ident[:])
                    m.then_inc(s_xfT, 1)
                pe.wait_ge(s_xfT_sb, 2)
                for t in range(TILES):
                    m = pe.matmul(bank(6, E, t * E), xfT[:, t * P:(t + 1) * P], gate_w[:], start=True, stop=True)
                m.then_inc(s_logits, 1)
                pe.wait_ge(s_counts, 1)
                pe.matmul(bank(7), before[:], counts, start=True, stop=False)
                for s in range(1, TILES):
                    m = pe.matmul(bank(7), ones[:], counts_pad[:, none_before - s * E:none_before + (TILES - s) * E],
                                  start=False, stop=(s == TILES - 1))
                m.then_inc(s_prefix, 1)
                pe.wait_ge(s_wts, 1)
                for i in range(2):
                    for k in range(4):
                        t = i * 4 + k
                        m = pe.transpose(bank(4 + i, P, k * P)[0:E, :], weights[:, t * E:(t + 1) * E], ident[:])
                    m.then_inc(s_wts_T, 1)
                for i in range(2):
                    pe.wait_ge(s_wts_sb, i + 1)
                    for k in range(4):
                        m = pe.matmul(bank(2 + i, D, k * D), weights_T[:, (i * 4 + k) * P:(i * 4 + k + 1) * P], b2_t[:],
                                      start=True, stop=True)
                    m.then_inc(s_b2, 1)
                pe.wait_ge(s_b2_added, 2)

                def x_transpose(p, slot, turn):
                    pe.wait_ge(s_xin[slot], (turn + 1) * 16)
                    reached(pe, s_xT, p - 1)
                    pe.transpose(bank(slot % 2, P), x_in[slot][:, 0:D], ident[:]).then_inc(s_xT_ps, 1)

                def layer1(p, slot, turn):
                    pe.wait_ge(s_xT, p + 1)
                    pe.wait_ge(s_w1[slot], (turn + 1) * 16)
                    reached(pe, s_h, p - 1)
                    for e in range(2):
                        m = pe.matmul(bank(2 + slot % 2)[e * CAP:(e + 1) * CAP, :], xT[slot % 2][:, e * CAP:(e + 1) * CAP],
                                      w1[slot][:, e, :], start=True, stop=True)
                    m.then_inc(s_h_ps, 1)

                def h_transpose(p, slot, turn):
                    pe.wait_ge(s_h, p + 1)
                    reached(pe, s_hc, p - 1)
                    rows = h_rows[slot % 2].rearrange("s (h c) -> s c h", c=HC)
                    for c in range(HC):
                        m = pe.transpose(bank(4 + slot % 2, P, c * P), rows[:, c, :], ident[:])
                    m.then_inc(s_hc_ps, 1)

                def layer2(p, slot, turn):
                    pe.wait_ge(s_gelu, p + 1)
                    pe.wait_ge(s_w2[slot], (turn + 1) * 16)
                    reached(pe, s_y, p - 1)
                    for c in range(HC):
                        for e in range(2):
                            m = pe.matmul(bank(6 + slot % 2, D)[e * CAP:(e + 1) * CAP, :],
                                          h_gelu[slot % 2][:, c * P + e * CAP:c * P + (e + 1) * CAP],
                                          w2[slot][:, e, c, :], start=(c == 0), stop=(c == HC - 1))
                    m.then_inc(s_y_ps, 1)

                pipeline(pe, [(0, x_transpose), (1, layer1), (2, h_transpose), (3, layer2)])


_OUTS = [((1, 1024, 128), "float32")]


def kernel(**inputs):
    import numpy as _np
    import concourse.bacc as _bacc
    from concourse import mybir as _mybir
    from concourse.bass_utils import run_bass_kernel_spmd as _run

    nc = _bacc.Bacc("TRN2", target_bir_lowering=False, num_devices=1)
    i = {k: _np.asarray(v) for k, v in inputs.items()}
    ctx_t = _np.zeros((D, SKP), _np.float32)
    ctx_t[:, :SK] = i["ctx_1024"][0].T
    arrays = {
        "x": i["x"],
        "ctx_t": ctx_t,
        "wq_t": i["L0_xattn_w_q"].reshape(NH, DK, D).transpose(2, 1, 0).reshape(D, D),
        "wk_t": i["L0_xattn_w_k"].reshape(NH, DK, D).transpose(2, 1, 0).reshape(D, D),
        "wv_t": i["L0_xattn_w_v"].T,
        "wo_t": i["L0_xattn_w_o"].T,
        "b_o": i["L0_xattn_b_o"],
        "gate_w": i["L0_ffn_gate_w"],
        "gate_b": i["L0_ffn_gate_b"],
        "w1": i["L0_ffn_w1"],
        "b1_t": i["L0_ffn_b1"].reshape(E, P, HC).transpose(1, 0, 2).reshape(P, E * HC),
        "w2": i["L0_ffn_w2"],
        "b2": i["L0_ffn_b2"],
        **constants(),
    }
    arrays = {k: _np.ascontiguousarray(v) for k, v in arrays.items()}
    aps = {k: nc.dram_tensor(f"in_{k}", v.shape, _mybir.dt.from_np(v.dtype), kind="ExternalInput").ap()
           for k, v in arrays.items()}
    shape, dtype = _OUTS[0]
    out = nc.dram_tensor("out", shape, _mybir.dt.from_np(_np.dtype(dtype)), kind="ExternalOutput").ap()
    build(nc, aps, out)
    r = _run(nc, [{f"in_{k}": v for k, v in arrays.items()}], core_ids=[0])
    return r.results[0]["out"]
```
